# Optimizing a Trainium2 kernel written in Bass

```python
import numpy as np
import jax
import jax.numpy as jnp

def _softmax(x, axis=-1):
    return jax.nn.softmax(x, axis=axis)

def _gelu(x):
    return jax.nn.gelu(x, approximate=True)

def _silu(x):
    return jax.nn.silu(x)

def _sigmoid(x):
    return jax.nn.sigmoid(x)

def _layernorm(x, axis=-1, eps=1e-05):
    m = jnp.mean(x, axis=axis, keepdims=True)
    v = jnp.var(x, axis=axis, keepdims=True)
    return (x - m) / jnp.sqrt(v + eps)

def _scatter_add(tgt, idx, src, axis=0):
    return tgt.at[idx].add(src)

def _segment_sum(src, seg, n):
    return jax.ops.segment_sum(src, seg, n)
kernel_name = 'mk_macaron_d1_jaxref_r8_6d3c77'

def setup_inputs(seed: int=0):
    np.random.seed(seed)
    _w = jnp.asarray

    def _L0_attn_setup():
        import jax, jax.numpy as jnp
        import numpy as np
        DIMS = 128
        HEAD = 16
        HD = DIMS // HEAD
        EPS = 1e-05

        def _freqs_base():
            hd2 = HD // 2
            top = 2595.0 * jnp.log10(jnp.asarray(1.0 + 4000.0 / 200.0, dtype=jnp.float32))
            mel = jnp.power(10.0, jnp.linspace(0.0, top, hd2, dtype=jnp.float32) / 2595.0) - 1.0
            return 200.0 * mel / 1000.0

        def _rope(x, theta):
            T = x.shape[2]
            freqs = theta / 220.0 * _freqs_base()
            ang = jnp.arange(T, dtype=jnp.float32)[:, None] * freqs
            cos, sin = (jnp.cos(ang), jnp.sin(ang))
            xr = x.reshape(*x.shape[:-1], HD // 2, 2)
            a, b = (xr[..., 0], xr[..., 1])
            rot = jnp.stack([a * cos - b * sin, a * sin + b * cos], axis=-1)
            return rot.reshape(x.shape).astype(x.dtype)

        def _taylor_softmax(x):
            t = 1.0 + x + 0.5 * x * x
            return t / jnp.sum(t, axis=-1, keepdims=True)
        key = jax.random.key(seed)
        ks = jax.random.split(key, 4)
        B, T = (1, 256)
        s = 1.0 / np.sqrt(DIMS)
        return {'x': jax.random.normal(ks[0], (B, T, DIMS), dtype=jnp.float32), 'ln_w': jnp.ones((DIMS,), dtype=jnp.float32), 'ln_b': jnp.zeros((DIMS,), dtype=jnp.float32), 'w_q': jax.random.normal(ks[1], (DIMS, DIMS), dtype=jnp.float32) * s, 'w_kv': jax.random.normal(ks[2], (DIMS, 2 * DIMS), dtype=jnp.float32) * s, 'w_o': jax.random.normal(ks[3], (DIMS, DIMS), dtype=jnp.float32) * s, 'theta': jnp.asarray(10000.0, dtype=jnp.float32)}
    _L0_attn_in = _L0_attn_setup()

    def _L0_ffn_setup():
        import jax, jax.numpy as jnp
        import numpy as np
        H = 128
        E = 64
        K = 8
        G = 8
        TOPK_GROUP = 4
        I_MOE = 64
        I_SHARED = 256
        SCALE = 2.5

        def relu2(x):
            return jnp.square(jax.nn.relu(x))

        def _route(xf, router_w, correction_bias):
            T = xf.shape[0]
            logits = xf @ router_w.T
            scores = jax.nn.sigmoid(logits)
            sfc = scores + correction_bias[None, :]
            grp = sfc.reshape(T, G, E // G)
            top2, _ = jax.lax.top_k(grp, 2)
            group_scores = top2.sum(-1)
            _, gidx = jax.lax.top_k(group_scores, TOPK_GROUP)
            gmask = jnp.zeros((T, G), sfc.dtype).at[jnp.arange(T)[:, None], gidx].set(1.0)
            emask = jnp.repeat(gmask, E // G, axis=1)
            masked = jnp.where(emask > 0, sfc, 0.0)
            _, tidx = jax.lax.top_k(masked, K)
            tw = jnp.take_along_axis(scores, tidx, axis=1)
            tw = tw / (tw.sum(-1, keepdims=True) + 1e-20)
            return (tidx, tw * SCALE)
        key = jax.random.key(seed)
        ks = jax.random.split(key, 7)
        x = jax.random.normal(ks[0], (2, 128, H), dtype=jnp.float32)
        router_w = jax.random.normal(ks[1], (E, H), dtype=jnp.float32) * 0.02
        correction_bias = jax.random.normal(ks[2], (E,), dtype=jnp.float32) * 0.01
        up_w = jax.random.normal(ks[3], (E, H, I_MOE), dtype=jnp.float32) * 0.02
        down_w = jax.random.normal(ks[4], (E, I_MOE, H), dtype=jnp.float32) * 0.02
        shared_up_w = jax.random.normal(ks[5], (H, I_SHARED), dtype=jnp.float32) * 0.02
        shared_down_w = jax.random.normal(ks[6], (I_SHARED, H), dtype=jnp.float32) * 0.02
        return {'x': x, 'router_w': router_w, 'correction_bias': correction_bias, 'up_w': up_w, 'down_w': down_w, 'shared_up_w': shared_up_w, 'shared_down_w': shared_down_w}
    _L0_ffn_in = _L0_ffn_setup()
    _d = {'L0_attn_x': _L0_attn_in['x'], 'L0_attn_ln_w': _L0_attn_in['ln_w'], 'L0_attn_ln_b': _L0_attn_in['ln_b'], 'L0_attn_w_q': _L0_attn_in['w_q'], 'L0_attn_w_kv': _L0_attn_in['w_kv'], 'L0_attn_w_o': _L0_attn_in['w_o'], 'L0_attn_theta': _L0_attn_in['theta'], 'L0_ffn_router_w': _L0_ffn_in['router_w'], 'L0_ffn_correction_bias': _L0_ffn_in['correction_bias'], 'L0_ffn_up_w': _L0_ffn_in['up_w'], 'L0_ffn_down_w': _L0_ffn_in['down_w'], 'L0_ffn_shared_up_w': _L0_ffn_in['shared_up_w'], 'L0_ffn_shared_down_w': _L0_ffn_in['shared_down_w']}
    _x0 = _d['L0_attn_x']
    _d['L0_attn_x'] = jax.random.normal(jax.random.fold_in(jax.random.key(seed), 1), (16, 256, 128), dtype=_x0.dtype)
    del _x0
    return _d

def reference(L0_attn_x, L0_attn_ln_w, L0_attn_ln_b, L0_attn_w_q, L0_attn_w_kv, L0_attn_w_o, L0_attn_theta, L0_ffn_router_w, L0_ffn_correction_bias, L0_ffn_up_w, L0_ffn_down_w, L0_ffn_shared_up_w, L0_ffn_shared_down_w):

    def _L0_attn_ref(x, ln_w, ln_b, w_q, w_kv, w_o, theta):
        import jax, jax.numpy as jnp
        import numpy as np
        DIMS = 128
        HEAD = 16
        HD = DIMS // HEAD
        EPS = 1e-05

        def _freqs_base():
            hd2 = HD // 2
            top = 2595.0 * jnp.log10(jnp.asarray(1.0 + 4000.0 / 200.0, dtype=jnp.float32))
            mel = jnp.power(10.0, jnp.linspace(0.0, top, hd2, dtype=jnp.float32) / 2595.0) - 1.0
            return 200.0 * mel / 1000.0

        def _rope(x, theta):
            T = x.shape[2]
            freqs = theta / 220.0 * _freqs_base()
            ang = jnp.arange(T, dtype=jnp.float32)[:, None] * freqs
            cos, sin = (jnp.cos(ang), jnp.sin(ang))
            xr = x.reshape(*x.shape[:-1], HD // 2, 2)
            a, b = (xr[..., 0], xr[..., 1])
            rot = jnp.stack([a * cos - b * sin, a * sin + b * cos], axis=-1)
            return rot.reshape(x.shape).astype(x.dtype)

        def _taylor_softmax(x):
            t = 1.0 + x + 0.5 * x * x
            return t / jnp.sum(t, axis=-1, keepdims=True)
        B, T, _ = x.shape
        mu = jnp.mean(x, axis=-1, keepdims=True)
        var = jnp.mean(jnp.square(x - mu), axis=-1, keepdims=True)
        h = (x - mu) * jax.lax.rsqrt(var + EPS) * ln_w + ln_b
        q = h @ w_q
        kv = h @ w_kv
        k, v = (kv[..., :DIMS], kv[..., DIMS:])

        def to_heads(t):
            return t.reshape(B, T, HEAD, HD).transpose(0, 2, 1, 3)
        q, k, v = (to_heads(q), to_heads(k), to_heads(v))
        scale = HD ** (-0.5)
        q = _rope(q, theta)
        k = _rope(k, theta)
        qk = jnp.einsum('bhkd,bhqd->bhkq', q, k) * scale
        attn = _taylor_softmax(qk)
        wv = jnp.einsum('bhkq,bhqd->bhkd', attn, v)
        wv = wv.transpose(0, 2, 1, 3).reshape(B, T, DIMS)
        return wv @ w_o

    def _L0_ffn_ref(x, router_w, correction_bias, up_w, down_w, shared_up_w, shared_down_w):
        import jax, jax.numpy as jnp
        import numpy as np
        H = 128
        E = 64
        K = 8
        G = 8
        TOPK_GROUP = 4
        I_MOE = 64
        I_SHARED = 256
        SCALE = 2.5

        def relu2(x):
            return jnp.square(jax.nn.relu(x))

        def _route(xf, router_w, correction_bias):
            T = xf.shape[0]
            logits = xf @ router_w.T
            scores = jax.nn.sigmoid(logits)
            sfc = scores + correction_bias[None, :]
            grp = sfc.reshape(T, G, E // G)
            top2, _ = jax.lax.top_k(grp, 2)
            group_scores = top2.sum(-1)
            _, gidx = jax.lax.top_k(group_scores, TOPK_GROUP)
            gmask = jnp.zeros((T, G), sfc.dtype).at[jnp.arange(T)[:, None], gidx].set(1.0)
            emask = jnp.repeat(gmask, E // G, axis=1)
            masked = jnp.where(emask > 0, sfc, 0.0)
            _, tidx = jax.lax.top_k(masked, K)
            tw = jnp.take_along_axis(scores, tidx, axis=1)
            tw = tw / (tw.sum(-1, keepdims=True) + 1e-20)
            return (tidx, tw * SCALE)
        B, S, Hd = x.shape
        xf = x.reshape(-1, Hd)
        T = xf.shape[0]
        tidx, tw = _route(xf.astype(jnp.float32), router_w, correction_bias)
        combine = jnp.zeros((T, E), xf.dtype).at[jnp.arange(T)[:, None], tidx].add(tw.astype(xf.dtype))

        def body(acc, ew):
            wu, wd, c = ew
            return (acc + c[:, None] * (relu2(xf @ wu) @ wd), None)
        routed, _ = jax.lax.scan(body, jnp.zeros_like(xf), (up_w, down_w, combine.T))
        shared = relu2(xf @ shared_up_w) @ shared_down_w
        return (routed + shared).reshape(B, S, Hd)
    x = L0_attn_x
    x = x + 0.5 * _L0_ffn_ref(_layernorm(x, axis=-1), L0_ffn_router_w, L0_ffn_correction_bias, L0_ffn_up_w, L0_ffn_down_w, L0_ffn_shared_up_w, L0_ffn_shared_down_w)
    x = x + _L0_attn_ref(_layernorm(x, axis=-1), L0_attn_ln_w, L0_attn_ln_b, L0_attn_w_q, L0_attn_w_kv, L0_attn_w_o, L0_attn_theta)
    x = x + 0.5 * _L0_ffn_ref(_layernorm(x, axis=-1), L0_ffn_router_w, L0_ffn_correction_bias, L0_ffn_up_w, L0_ffn_down_w, L0_ffn_shared_up_w, L0_ffn_shared_down_w)
    return x

_drawn_inputs = setup_inputs


def setup_inputs(seed=0):
    import zlib

    import numpy as np

    out = dict(_drawn_inputs(seed))
    spreads = {'L0_attn_ln_w': (1.0, 0.554), 'L0_attn_ln_b': (0.0, 0.1)}
    factors = {'L0_ffn_router_w': 7.186,
     'L0_ffn_correction_bias': 8.0,
     'L0_ffn_up_w': 7.266,
     'L0_ffn_down_w': 6.621,
     'L0_ffn_shared_up_w': 3.169,
     'L0_ffn_shared_down_w': 2.84}
    for name, (base, spread) in spreads.items():
        noise = np.random.default_rng([zlib.crc32(name.encode()), seed]).standard_normal(out[name].shape)
        drawn = base * np.exp(spread * noise) if base else spread * noise
        out[name] = jnp.asarray(drawn.astype(out[name].dtype))
    for name, factor in factors.items():
        out[name] = (out[name] * factor).astype(out[name].dtype)
    return out
```

```python
from contextlib import ExitStack

import concourse.bass as bass
import numpy as np
from concourse import mybir

F32 = mybir.dt.float32
F32R = mybir.dt.float32r
I32 = mybir.dt.int32
ALU = mybir.AluOpType
ACT = mybir.ActivationFunctionType
AX_X = mybir.AxisListType.X

P = 128
D = 128
TOKENS = 4096
TILE = 512
SUB = TILE // P
TILES = TOKENS // TILE
E = 64
I_MOE = 64
G = 8
GE = E // G
TOPK_GROUP = 4
SCALE = 2.5
I_SHARED = 256
RC = E * I_MOE // P
SC = I_SHARED // P
NC = RC + SC
LAG = 4
BY_VECTOR = (1, 3, 5, 8, 18, 32)
BY_SCALAR = tuple(c for c in range(NC) if c not in BY_VECTOR)
PIECES = [(0, 8), (8, 16), (16, 24), (24, NC)]
EPS = 1e-5

T = 256
BATCHES = TOKENS // T
BS = T // P
HEADS = 16
HD = 8
ND = 5
NF = ND + 1
VW = D + HEADS
EXT = 12
NEG = -3.0e38

TWO_PI = 6.283185307179586
TWO_PI_PARTS = (6.28125, 0.0019350051879882812, 3.0199159819567e-07)
ROUND = 12582912.0
PI_BELOW = 3.1415925


def bc(ap, axis, shape):
    return ap.unsqueeze(axis).to_broadcast(shape)


class Own:

    def __init__(self, eng, sem):
        self.eng, self.sem, self.n = eng, sem, 0

    def done(self, instruction):
        self.n += 1
        instruction.then_inc(self.sem, 1)
        self.eng.wait_ge(self.sem, self.n)

    def clear(self):
        if self.n:
            self.eng.sem_clear(self.sem)
            self.n = 0


class Step:

    def __init__(self, h, u):
        self.h, self.u, self.n = h, u, 2 * h + u

    def next(self):
        return Step(self.h, 1) if self.u == 0 else Step(self.h + 1, 0)

    def prev(self):
        return Step(self.h, 0) if self.u == 1 else Step(self.h - 1, 1)


def wait(eng, sem, value):
    if not isinstance(value, int) or value > 0:
        eng.wait_ge(sem, value)


def rsqrt_estimate(v, own, y, a):
    own.done(v.tensor_scalar(y.bitcast(I32), a.bitcast(I32), -0.5, float(0x5F3759DF), ALU.mult, ALU.add))


def rsqrt_newton(v, own, y, tmp, a):
    own.done(v.tensor_tensor(tmp, y, y, ALU.mult))
    own.done(v.scalar_tensor_tensor(out=tmp, in0=tmp, scalar=-0.5, in1=a, op0=ALU.mult, op1=ALU.mult))
    own.done(v.scalar_tensor_tensor(out=y, in0=tmp, scalar=1.5, in1=y, op0=ALU.add, op1=ALU.mult))


def build(nc, x, ln_w, ln_b, w_q, w_qs, w_k, w_ks, w_v, w_o, theta, router_wT, bias, up_w, down_w,
          s_up, s_down, ident_in, ident2_in, lower_in, shift_in, mask_in, pos_in, base_in, sign_in, out):
    x1 = nc.dram_tensor("x_after_ffn1", (TOKENS, D), F32).ap()
    x2 = nc.dram_tensor("x_after_attn", (TOKENS, D), F32).ap()

    with ExitStack() as ctx:
        def sb(name, shape, dt=F32):
            return ctx.enter_context(nc.sbuf_tensor(name, shape, dt))

        def sem(name):
            return ctx.enter_context(nc.semaphore(name))

        banks = ctx.enter_context(nc.psum_tensor("banks", [P, 8, 512], F32))
        bank = [banks[:, i] for i in range(8)]

        up_hi = sb("up_hi", [P, NC, P], F32R)
        up_lo = sb("up_lo", [P, NC, P], F32R)
        down_hi = sb("down_hi", [P, NC, P], F32R)
        down_lo = sb("down_lo", [P, NC, P], F32R)
        up_raw = sb("up_raw", [P, NC, P])
        down_raw = sb("down_raw", [P, NC, P])
        sel = sb("sel", [P, E, I_MOE], F32R)
        rw = sb("rw", [P, E])
        biasB = sb("biasB", [P, E])
        ident = sb("ident", [P, P])
        ident2 = sb("ident2", [P, E])
        lower = sb("lower", [P, G, G])
        wq = sb("wq", [P, 2, D])
        wkv = sb("wkv", [P, 3, D])
        wo = sb("wo", [P, D])
        lnw = sb("lnw", [P, 1])
        lnb = sb("lnb", [P, 1])
        shift = sb("shift", [P, ND - 1, P], F32R)
        mask = sb("mask", [P, NF, VW])
        ones = sb("ones", [P, P])
        th = sb("th", [P, 8])

        xt = sb("xt", [P, 2, SUB, D])
        xo = sb("xo", [P, 2, SUB, D])
        stats = sb("stats", [P, SUB, 6])
        mv = sb("mv", [P, SUB, 2])
        small = sb("small", [P, 8, SUB])
        xn = sb("xn", [P, SUB, D])
        xTf = sb("xTf", [P, TILE])
        xT_hi = sb("xT_hi", [P, 2, TILE], F32R)
        xT_lo = sb("xT_lo", [P, 2, TILE], F32R)
        cT = sb("cT", [P, 2, TILE], F32R)
        scores = sb("scores", [P, SUB, E])
        sfc = sb("sfc", [P, SUB * G, GE])
        hi1 = sb("hi1", [P, SUB * G, 4])
        lo1 = sb("lo1", [P, SUB * G, 4])
        hi2 = sb("hi2", [P, SUB * G, 2])
        lo2 = sb("lo2", [P, SUB * G, 2])
        mn = sb("mn", [P, SUB * G, 2])
        gsc = sb("gsc", [P, SUB, G])
        cmpb = sb("cmpb", [P, SUB, G, G])
        gmask = sb("gmask", [P, SUB * G])
        top8 = sb("top8", [P, SUB, 8])
        rest = sb("rest", [P, SUB, E])
        cmpa, comb = rest[:].rearrange("p s (g e) -> p s g e", e=G), rest
        cc = sb("cc", [P, SUB, 2, E], F32R)
        NR, NG = 2, 4
        work = sb("work", [P, (2 * NR + NG) * TILE])
        cuts = [work[:, k * TILE:(k + 1) * TILE] for k in range(2 * NR + NG)]
        r, sq, g = cuts[0:NR], cuts[NR:2 * NR], cuts[2 * NR:]
        g_hi = sb("g_hi", [P, NG, TILE], F32R)
        g_lo = sb("g_lo", [P, NG, TILE], F32R)
        acc = xn[:].rearrange("p s d -> p (s d)")
        tabs = sb("tabs", [P, 4, T])
        tab_k = tabs[:, 0:2].rearrange("p s (w d) -> p s w d", w=2)
        tab_q = tabs[:, 2:4]
        trig = sb("trig", [P, 4, 2, T])
        warm = sb("warm", [P, 1])
        th_hi = sb("th_hi", [P, 1], F32R)

        def room(raw, shapes):
            flat, at, views = raw, 0, []
            for names, dims in shapes:
                n = int(np.prod(list(dims.values())))
                views.append(flat[:, at:at + n].rearrange(f"p ({names}) -> p {names}", **dims))
                at += n
            return views

        pair = ("u s d", dict(u=2, s=BS, d=D))
        xa, xr, xs, hn, hT, q_parts, qr, k_parts = room(down_raw[:].rearrange("p c d -> p (c d)"), [
            pair, pair, pair, pair, ("u t", dict(u=2, t=T)), ("w t", dict(w=2, t=T)), ("u t", dict(u=2, t=T)),
            ("s w d", dict(s=BS, w=2, d=D))])
        qf, at, atT = room(up_raw[:].rearrange("p c d -> p (c d)"), [("u f t", dict(u=2, f=NF, t=T)), pair, ("u t", dict(u=2, t=T))])
        a_stats = sb("a_stats", [P, BS, 6])
        a_mv = sb("a_mv", [P, BS, 2])
        a_small = sb("a_small", [P, 8, BS])
        k_ext = sb("k_ext", [P, BS, HEADS, EXT])
        kf, va_odd = room(work, [("u s f d", dict(u=2, s=BS, f=NF, d=D)), ("s w", dict(s=BS, w=VW))])
        va = [sb("va_even", [P, BS, VW])[:], va_odd]
        q_hi, q_lo = g_hi[:, 0:2, 0:T], g_hi[:, 2:4, 0:T]
        total, = room(xt[:, 1].rearrange("p s d -> p (s d)"), [("s w", dict(s=BS, w=VW))])
        rmat, sums = room(trig[:].rearrange("p k a t -> p (k a t)"), [
            ("u f w", dict(u=2, f=NF, w=VW)), ("u w", dict(u=2, w=VW))])
        shift_in_room = xo[:, 1]
        rz = sb("rz", [P, BS, HEADS])

        load_of = {n: sem(f"load_{n}") for n in
                   ["early", "table", "attn"] + [f"up{k}" for k in range(len(PIECES))] +
                   [f"down{k}" for k in range(len(PIECES))]}
        sel_ready = sem("sel_ready")
        up_hi_ready = sem("up_hi_ready")
        up_lo_ready = sem("up_lo_ready")
        down_hi_ready = sem("down_hi_ready")
        down_lo_ready = sem("down_lo_ready")
        ones_ready = sem("ones_ready")
        dve_own = sem("dve_own")

        def ffn_sems(tag):
            names = ["x_in0", "x_in1", "xn", "xTp", "xTf", "xsplit", "logits", "sig", "comb", "ccT", "cT", "up", "cb",
                     "relu", "sq", "g", "g_hi", "g_hiv", "g_lo", "down", "acc", "outT", "xo", "stored0", "stored1"]
            return {n: sem(f"{tag}_{n}") for n in names}

        S1 = ffn_sems("f1")
        S2 = ffn_sems("f2")
        A = {n: sem(f"at_{n}") for n in
             ["x_in0", "x_in1", "xr_in0", "xr_in1", "hn", "hTp", "hT", "qp", "kvp", "v", "q_read", "k_read",
              "qrot", "k_ext", "k_lin", "sq", "kf", "shift_a", "shift_b", "qf_a", "qf_b", "state", "sums", "rmat", "out_read", "q_hi", "q_lo",
              "outp", "at", "atTp", "atT", "yp", "xo", "stored0", "stored1"]}
        trig_ready = sem("trig_ready")
        sin_ready = sem("sin_ready")
        shift_ready = sem("shift_ready")

        ACC = [bank[1], bank[7]]
        XT = bank[0]
        LG = bank[2]
        CT = bank[2]
        CB = [bank[3], bank[6]]
        H = [bank[4], bank[5]]

        FIRST, LAST = Step(0, 0), Step(TILES // 2 - 1, 1)

        def load_x(sp, S, src, t):
            wait(sp, S["xo"], t.n - 1)
            sp.dma_start(xt[:, t.u], src_tile(src, t)).then_inc(S[f"x_in{t.u}"], 16)

        def src_tile(ap, t):
            return ap.rearrange("(n p) d -> p n d", p=P)[:, bass.ds(t.n * SUB, SUB), :]

        def store_x(sp, S, dst, t):
            sp.wait_ge(S["xo"], t.n + 1)
            sp.dma_start(src_tile(dst, t), xo[:, t.u]).then_inc(S[f"stored{t.u}"], 16)

        def sp_ffn_tile(sp, S, src, dst, t, first, last):
            if not first:
                store_x(sp, S, dst, t.prev())
            if not last:
                load_x(sp, S, src, t.next())
            elif S is S1:
                sp.wait_ge(S1["stored0"], 16 * 2)
                sp_load_a(sp, Step(0, 0))
                sp_load_a(sp, Step(0, 1))

        def dve_norm(dve, S, t, own, part):
            ve = nc.vector
            rstd, tmp, var = small[:, 1], small[:, 2], small[:, 0]
            if part == 0:
                dve.wait_ge(S[f"x_in{t.u}"], 16 * (t.h + 1))
                for s in range(SUB):
                    i = ve.bn_stats(out=stats[:, s], in_=xt[:, t.u, s])
                own.done(i)
            if part == 1:
                for s in range(SUB):
                    i = ve.bn_aggr(out=mv[:, s], in_=stats[:, s])
                own.done(i)
                own.done(ve.tensor_scalar(var, mv[:, :, 1], EPS, None, ALU.add))
                rsqrt_estimate(ve, own, rstd, var)
            if part == 2:
                rsqrt_newton(ve, own, rstd, tmp, var)
                rsqrt_newton(ve, own, rstd, tmp, var)
            if part == 3:
                rsqrt_newton(ve, own, rstd, tmp, var)
            if part == 4:
                wait(dve, S["xTp"], t.n)
                for s in range(SUB):
                    i = ve.tensor_scalar(xn[:, s], xt[:, t.u, s], mv[:, s, 0:1], small[:, 1, s:s + 1],
                                         ALU.subtract, ALU.mult)
                i.then_inc(S["xn"], 1)

        def dve_split_x(dve, S, t, own, part):
            ve = nc.vector
            if part == 0:
                dve.wait_ge(S["xTf"], t.n + 1)
                wait(dve, S["up"], (t.n - 1) * NC)
                own.done(ve.tensor_copy(xT_hi[:, t.u], xTf[:]))
            if part == 1:
                ve.tensor_tensor(xT_lo[:, t.u], xTf[:], xT_hi[:, t.u].bitcast(F32), ALU.subtract)\
                    .then_inc(S["xsplit"], 1)

        def dve_route(dve, S, t, own, part):
            ve = nc.vector
            m = sfc[:].rearrange("p (s g) e -> p s (g e)", s=SUB)
            if part == 0:
                dve.wait_ge(S["sig"], t.n + 1)
                own.done(ve.tensor_tensor(m, scores[:], bc(biasB[:], 1, [P, SUB, E]), ALU.add))
            if part == 1:
                ve.tensor_tensor(hi1[:], sfc[:, :, 0:4], sfc[:, :, 4:8], ALU.max)
                own.done(ve.tensor_tensor(lo1[:], sfc[:, :, 0:4], sfc[:, :, 4:8], ALU.min))
                ve.tensor_tensor(hi2[:], hi1[:, :, 0:2], hi1[:, :, 2:4], ALU.max)
                ve.tensor_tensor(mn[:], hi1[:, :, 0:2], hi1[:, :, 2:4], ALU.min)
                own.done(ve.tensor_tensor(lo2[:], lo1[:, :, 0:2], lo1[:, :, 2:4], ALU.max))
            if part == 2:
                own.done(ve.tensor_tensor(lo2[:], lo2[:], mn[:], ALU.max))
                ve.tensor_tensor(hi1[:, :, 0:1], hi2[:, :, 0:1], hi2[:, :, 1:2], ALU.max)
                ve.tensor_tensor(mn[:, :, 0:1], hi2[:, :, 0:1], hi2[:, :, 1:2], ALU.min)
                own.done(ve.tensor_tensor(lo1[:, :, 0:1], lo2[:, :, 0:1], lo2[:, :, 1:2], ALU.max))
                own.done(ve.tensor_tensor(lo1[:, :, 0:1], lo1[:, :, 0:1], mn[:, :, 0:1], ALU.max))
                gs = gsc[:].rearrange("p s g -> p (s g)").unsqueeze(2)
                own.done(ve.tensor_tensor(gs, hi1[:, :, 0:1], lo1[:, :, 0:1], ALU.add))
            other = bc(gsc[:], 2, [P, SUB, G, G])
            mine = bc(gsc[:], 3, [P, SUB, G, G])
            if part == 3:
                own.done(ve.tensor_tensor(cmpb[:], other, mine, ALU.is_equal))
                ve.tensor_tensor(cmpa, other, mine, ALU.is_gt)
            if part == 4:
                own.done(ve.tensor_tensor(cmpb[:], cmpb[:], bc(lower[:], 1, [P, SUB, G, G]), ALU.mult))
                own.done(ve.tensor_tensor(cmpa, cmpa, cmpb[:], ALU.add))
            if part == 5:
                own.done(ve.tensor_reduce(out=gmask[:].rearrange("p (s g) -> p s g", s=SUB), in_=cmpa,
                                          axis=AX_X, op=ALU.add))
                own.done(ve.tensor_scalar(gmask[:], gmask[:], TOPK_GROUP - 0.5, None, ALU.is_lt))
                own.done(ve.tensor_tensor(sfc[:], sfc[:], bc(gmask[:], 2, [P, SUB * G, GE]), ALU.mult))
            if part == 6:
                for s in range(SUB):
                    i = ve.max(top8[:, s], m[:, s])
                own.done(i)
            if part in (7, 8):
                for s in range(SUB // 2 * (part - 7), SUB // 2 * (part - 6)):
                    i = ve.match_replace(out=rest[:, s], in_to_replace=top8[:, s], in_values=m[:, s], imm_value=NEG)
                own.done(i)
            if part == 9:
                own.done(ve.scalar_tensor_tensor(out=comb[:], in0=rest[:], scalar=NEG / 2, in1=scores[:],
                                                 op0=ALU.is_lt, op1=ALU.mult))
                own.done(ve.tensor_reduce(out=small[:, 3], in_=comb[:], axis=AX_X, op=ALU.add))
            if part == 10:
                own.done(ve.tensor_scalar(small[:, 3], small[:, 3], 1e-20, None, ALU.add))
                own.done(ve.reciprocal(small[:, 4], small[:, 3]))
                own.done(ve.tensor_scalar(small[:, 4], small[:, 4], 0.5 * SCALE, None, ALU.mult))
                own.done(ve.tensor_tensor(comb[:], comb[:], bc(small[:, 4], 2, [P, SUB, E]), ALU.mult))
            if part == 11:
                wait(dve, S["ccT"], t.n)
                own.done(ve.tensor_copy(cc[:, :, 0], comb[:]))
                ve.tensor_tensor(cc[:, :, 1], comb[:], cc[:, :, 0].bitcast(F32), ALU.subtract)\
                    .then_inc(S["comb"], 1)

        def dve_residual(dve, S, t):
            dve.wait_ge(S["outT"], t.n + 1)
            dve.wait_ge(S[f"stored{t.u}"], 16 * (t.h + 1))
            nc.vector.tensor_tensor(xo[:, t.u].rearrange("p s d -> p (s d)"), XT,
                                    xt[:, t.u].rearrange("p s d -> p (s d)"), ALU.add).then_inc(S["xo"], 1)

        def buf(t, c, count):
            return (t.u * NC + c) % count

        def high_made(t, c):
            name, chunks = ("g_hiv", BY_VECTOR) if c in BY_VECTOR else ("g_hi", BY_SCALAR)
            return name, t.n * len(chunks) + chunks.index(c) + 1

        def dve_weigh(dve, S, t, c):
            n = t.n * NC + c
            dve.wait_ge(S["sq"], n + 1)
            wait(dve, S["g_lo"], n + 1 - NG)
            src, dst = sq[buf(t, c, NR)], g[buf(t, c, NG)]
            if c < RC:
                dve.wait_ge(S["cb"], t.n * RC + c + 1)
                nc.vector.tensor_tensor(dst, src, CB[c % 2], ALU.mult).then_inc(S["g"], 1)
            else:
                nc.vector.tensor_scalar(dst, src, 0.5, None, ALU.mult).then_inc(S["g"], 1)

        def dve_high(dve, S, t, c):
            n = t.n * NC + c
            dve.wait_ge(S["g"], n + 1)
            wait(dve, S["down"], n + 1 - NG)
            nc.vector.tensor_copy(g_hi[:, buf(t, c, NG)], g[buf(t, c, NG)]).then_inc(S["g_hiv"], 1)

        NORM_AT = (10, 11, 12, 13, 14)
        SPLIT_AT = (16, 17)
        ROUTE_AT = tuple(range(19, 31))

        def dve_ffn_tile(dve, S, t, first, last, own):
            for c in range(NC):
                dve_weigh(dve, S, t, c)
                if c in BY_VECTOR:
                    dve_high(dve, S, t, c)
                if first and S is S1:
                    dve_trig_part(dve, c, own)
                if last and S is S1 and 11 <= c < 16:
                    dve_a_norm(dve, Step(0, 0), own, c - 11)
                if last and S is S1 and 17 <= c < 22:
                    dve_a_norm(dve, Step(0, 1), own, c - 17)
                if last and S is S1 and 24 <= c < 27:
                    dve_a_rotate(dve, FIRST, own, c - 24)
                if c == LAG + 3 and not first:
                    dve_residual(dve, S, t.prev())
                if last:
                    continue
                if c in NORM_AT:
                    dve_norm(dve, S, t.next(), own, NORM_AT.index(c))
                if c in SPLIT_AT:
                    dve_split_x(dve, S, t.next(), own, SPLIT_AT.index(c))
                if c in ROUTE_AT:
                    dve_route(dve, S, t.next(), own, ROUTE_AT.index(c))
            own.clear()

        def dve_parts(part_of, parts, dve, S, t, own):
            for part in parts:
                part_of(dve, S, t, own, part)

        def act_xTf(act, S, t):
            act.wait_ge(S["xTp"], t.n + 1)
            wait(act, S["logits"], t.n)
            wait(act, S["xsplit"], t.n)
            nc.scalar.activation(xTf[:], XT, ACT.Copy).then_inc(S["xTf"], 1)

        def act_sigmoid(act, S, t):
            act.wait_ge(S["logits"], t.n + 1)
            wait(act, S["comb"], t.n)
            nc.scalar.activation(scores[:].rearrange("p s e -> p (s e)"), LG[:, 0:SUB * E],
                                 ACT.Sigmoid).then_inc(S["sig"], 1)

        def act_cT(act, S, t):
            act.wait_ge(S["ccT"], t.n + 1)
            wait(act, S["cb"], (t.n - 1) * RC)
            nc.scalar.activation(cT[:, t.u], CT, ACT.Copy).then_inc(S["cT"], 1)

        def act_acc(act, S, t):
            act.wait_ge(S["down"], (t.n + 1) * NC)
            nc.scalar.activation(acc, ACC[t.u], ACT.Copy).then_inc(S["acc"], 1)

        def act_relu(act, S, t, c):
            n = t.n * NC + c
            act.wait_ge(S["up"], n + 1)
            wait(act, S["sq"], n + 1 - NR)
            nc.scalar.activation(r[buf(t, c, NR)], H[c % 2], ACT.Relu).then_inc(S["relu"], 1)

        def act_square(act, S, t, c):
            n = t.n * NC + c
            act.wait_ge(S["relu"], n + 1)
            wait(act, S["g"], n + 1 - NR)
            nc.scalar.activation(sq[buf(t, c, NR)], r[buf(t, c, NR)], ACT.Square).then_inc(S["sq"], 1)

        def act_high(act, S, t, c):
            if c in BY_VECTOR:
                return
            n = t.n * NC + c
            act.wait_ge(S["g"], n + 1)
            wait(act, S["down"], n + 1 - NG)
            nc.scalar.activation(g_hi[:, buf(t, c, NG)], g[buf(t, c, NG)], ACT.Copy).then_inc(S["g_hi"], 1)

        def act_ffn_tile(act, S, t, first, last):
            for c in range(NC):
                act_relu(act, S, t, c)
                if c >= 2:
                    act_high(act, S, t, c - 2)
                elif not first:
                    act_high(act, S, t.prev(), NC - 2 + c)
                act_square(act, S, t, c)
                if first and S is S1:
                    act_setup_part(act, c)
                if c == LAG and not first:
                    act_acc(act, S, t.prev())
                if last:
                    if S is S1 and c == 21:
                        act.wait_ge(load_of["attn"], 16 * 10)
                        act_a_hT(act, FIRST)
                    continue
                if c == 17:
                    act_xTf(act, S, t.next())
                if c == 19:
                    act_sigmoid(act, S, t.next())
                if c == 33:
                    act_cT(act, S, t.next())
            if last:
                act_high(act, S, t, NC - 2)
                act_high(act, S, t, NC - 1)

        def pool_ffn_tile(pool, S, t, first):
            for c in range(NC):
                n = t.n * NC + c
                made, count = high_made(t, c)
                pool.wait_ge(S[made], count)
                wait(pool, S["down"], n + 1 - NG)
                b = buf(t, c, NG)
                nc.gpsimd.tensor_tensor(g_lo[:, b], g[b], g_hi[:, b].bitcast(F32), ALU.subtract)\
                    .then_inc(S["g_lo"], 1)
                if first and S is S1 and c in (4, 10):
                    pool_low(pool, down_raw, down_hi, down_lo, down_hi_ready, down_lo_ready, (c + 8) // 6)

        def pe_transpose_x(pe, S, t):
            pe.wait_ge(S["xn"], t.n + 1)
            wait(pe, S["xo"], t.n - 1)
            for s in range(SUB):
                i = nc.tensor.transpose(XT[:, s * P:(s + 1) * P], xn[:, s], ident[:])
            i.then_inc(S["xTp"], 1)

        def pe_router(pe, S, t):
            pe.wait_ge(S["xTf"], t.n + 1)
            wait(pe, S["cT"], t.n)
            for s in range(SUB):
                i = nc.tensor.matmul(LG[:, s * E:(s + 1) * E], xTf[:, s * P:(s + 1) * P], rw[:],
                                     start=True, stop=True)
            i.then_inc(S["logits"], 1)

        def pe_transpose_c(pe, S, t):
            pe.wait_ge(S["comb"], t.n + 1)
            wait(pe, S["sig"], t.n + 1)
            for s in range(SUB):
                i = nc.tensor.transpose(CT[:, s * P:(s + 1) * P],
                                        cc[:, s].rearrange("p a e -> p (a e)").bitcast(F32), ident[:])
            i.then_inc(S["ccT"], 1)

        def pe_transpose_out(pe, S, t):
            pe.wait_ge(S["acc"], t.n + 2)
            wait(pe, S["xTf"], t.n + 1)
            for s in range(SUB):
                i = nc.tensor.transpose(XT[:, s * P:(s + 1) * P], acc[:, s * P:(s + 1) * P], ident[:])
            i.then_inc(S["outT"], 1)

        def pe_down(pe, S, t, c):
            n = t.n * NC + c
            pe.wait_ge(S["g_lo"], n + 1)
            if c == 0:
                wait(pe, S["acc"], t.n)
            if isinstance(t.n, int) and t.n == 0 and S is S1 and c in starts:
                pe.wait_ge(down_lo_ready, 1 + starts.index(c))
            b = buf(t, c, NG)
            nc.tensor.matmul(ACC[t.u], down_hi[:, c], g_hi[:, b], start=(c == 0), stop=False)
            nc.tensor.matmul(ACC[t.u], down_hi[:, c], g_lo[:, b], start=False, stop=False)
            nc.tensor.matmul(ACC[t.u], down_lo[:, c], g_hi[:, b], start=False, stop=(c == NC - 1))\
                .then_inc(S["down"], 1)

        starts = [a for a, _ in PIECES]

        def pe_ffn_tile(pe, S, t, first, last):
            for c in range(NC):
                n = t.n * NC + c
                if c == 0:
                    pe.wait_ge(S["xsplit"], t.n + 1)
                wait(pe, S["relu"], n - 1)
                if first and S is S1 and c in starts:
                    pe.wait_ge(up_lo_ready, 1 + starts.index(c))
                nc.tensor.matmul(H[c % 2], up_hi[:, c], xT_hi[:, t.u], start=True, stop=False)
                nc.tensor.matmul(H[c % 2], up_hi[:, c], xT_lo[:, t.u], start=False, stop=False)
                nc.tensor.matmul(H[c % 2], up_lo[:, c], xT_hi[:, t.u], start=False, stop=True)\
                    .then_inc(S["up"], 1)
                if c >= LAG:
                    pe_down(pe, S, t, c - LAG)
                elif not first:
                    pe_down(pe, S, t.prev(), NC - LAG + c)
                if c < RC:
                    if c == 0:
                        pe.wait_ge(S["cT"], t.n + 1)
                    wait(pe, S["g"], n - 1)
                    nc.tensor.matmul(CB[c % 2], sel[:, 2 * c:2 * c + 2].rearrange("p a b -> p (a b)"), cT[:, t.u],
                                     start=True, stop=True).then_inc(S["cb"], 1)
                if c == LAG + 2 and not first:
                    pe_transpose_out(pe, S, t.prev())
                if last:
                    if S is S1 and c == 20:
                        pe.wait_ge(S1["xo"], TILES - 1)
                        pe_a_hT(pe, FIRST)
                    if S is S1 and c == 23:
                        pe.wait_ge(S1["acc"], TILES)
                        pe.wait_ge(S1["cT"], TILES)
                        pe.wait_ge(load_of["attn"], 16 * 10)
                        pe_a_qkv(pe, FIRST)
                    continue
                if c == 16:
                    pe_transpose_x(pe, S, t.next())
                if c == 18:
                    pe_router(pe, S, t.next())
                if c == 33:
                    pe_transpose_c(pe, S, t.next())

        def ffn_tiles(eng, step):
            step(FIRST, True, False)
            with eng.Fori(0, (TILES - 2) // 2) as it:
                step(Step(it, 1), False, False)
                step(Step(it + 1, 0), False, False)
            step(LAST, False, True)

        def sp_ffn(sp, S, src, dst):
            ffn_tiles(sp, lambda t, first, last: sp_ffn_tile(sp, S, src, dst, t, first, last))
            store_x(sp, S, dst, LAST)

        def act_ffn(act, S):
            act.sem_inc(S["acc"], 1)
            ffn_tiles(act, lambda t, first, last: act_ffn_tile(act, S, t, first, last))

        def dve_ffn(dve, S, own):
            ffn_tiles(dve, lambda t, first, last: dve_ffn_tile(dve, S, t, first, last, own))

        def pool_ffn(pool, S):
            ffn_tiles(pool, lambda t, first, last: pool_ffn_tile(pool, S, t, first))

        def pe_ffn_end(pe, S):
            for c in range(NC - LAG, NC):
                pe_down(pe, S, LAST, c)
            pe_transpose_out(pe, S, LAST)

        AT = banks[:, 3, 0:T]
        T0 = banks[:, 0, 0:T]
        Q = banks[:, 0].rearrange("p (w t) -> p w t", w=2)
        KV = banks[:, 1:3]
        Y = AT.rearrange("p (s d) -> p s d", s=BS)
        ST = banks[:, 4:6, 0:NF // 2 * (D + 1)].rearrange("p b (f w) -> p b f w", w=D + 1)
        QS = banks[:, 6].rearrange("p (w t) -> p w t", w=2)
        OUT = banks[:, 7, 0:BS * VW].rearrange("p (s w) -> p s w", s=BS)
        SUMS = banks[:, 7, BS * VW:(BS + 1) * VW]

        def tokens_of(ap, t):
            return ap.rearrange("(n p) d -> p n d", p=P)[:, bass.ds(t.n * BS, BS), :]

        def sp_load_a(sp, t):
            wait(sp, A["hn"], t.n - 1)
            sp.dma_start(xa[:, t.u], tokens_of(x1, t)).then_inc(A[f"x_in{t.u}"], 16)

        def sp_load_r(sp, t):
            wait(sp, A["xo"], t.n - 1)
            sp.dma_start(xr[:, t.u], tokens_of(x1, t)).then_inc(A[f"xr_in{t.u}"], 16)

        def sp_store(sp, t):
            sp.wait_ge(A["xo"], t.n + 1)
            sp.dma_start(tokens_of(x2, t), xs[:, t.u]).then_inc(A[f"stored{t.u}"], 16)

        def dve_a_norm(dve, t, own, part):
            ve = nc.vector
            var, both, rstd, tmp = a_mv[:, :, 1], a_small[:, 0], a_small[:, 1], a_small[:, 3]
            if part == 0:
                dve.wait_ge(A[f"x_in{t.u}"], 16 * (t.h + 1))
                for s in range(BS):
                    i = ve.bn_stats(out=a_stats[:, s], in_=xa[:, t.u, s])
                own.done(i)
                for s in range(BS):
                    i = ve.bn_aggr(out=a_mv[:, s], in_=a_stats[:, s])
                own.done(i)
            if part == 1:
                own.done(ve.tensor_scalar(tmp, var, EPS, EPS, ALU.add, ALU.mult))
                own.done(ve.tensor_tensor(both, tmp, var, ALU.add))
                rsqrt_estimate(ve, own, rstd, both)
            if part == 2:
                rsqrt_newton(ve, own, rstd, tmp, both)
                rsqrt_newton(ve, own, rstd, tmp, both)
            if part == 3:
                rsqrt_newton(ve, own, rstd, tmp, both)
            if part == 4:
                wait(dve, A["hTp"], t.n - 1)
                for s in range(BS):
                    i = ve.tensor_scalar(hn[:, t.u, s], xa[:, t.u, s], a_mv[:, s, 0:1], a_small[:, 1, s:s + 1],
                                         ALU.subtract, ALU.mult)
                i.then_inc(A["hn"], 1)

        def dve_a_rotate(dve, t, own, part):
            ve = nc.vector
            if part == 0:
                dve.wait_ge(A["qp"], t.n + 1)
                ve.tensor_tensor(q_parts[:], Q, tab_q, ALU.mult).then_inc(A["q_read"], 1)
                dve.wait_ge(A["q_read"], t.n + 1)
                wait(dve, A["qf_b"], t.n - 1)
                wait(dve, A["sq"], t.n - 1)
                wait(dve, A["q_lo"], t.n - 1)
                ve.tensor_tensor(qr[:, t.u], q_parts[:, 0], q_parts[:, 1], ALU.add).then_inc(A["qrot"], 1)
            if part == 1:
                dve.wait_ge(A["kvp"], t.n + 1)
                ve.tensor_tensor(k_parts[:].rearrange("p s w d -> p s (w d)"), KV[:, :, 0:2 * D],
                                 tabs[:, 0:2], ALU.mult).then_inc(A["k_read"], 1)
            if part == 2:
                dve.wait_ge(A["k_read"], t.n + 1)
                wait(dve, A["k_lin"], t.n)
                wait(dve, A["kf"], t.n)
                heads = k_parts[:].rearrange("p s w (h e) -> p s w h e", e=HD)
                own.done(ve.tensor_tensor(k_ext[:, :, :, 0:HD], heads[:, :, 0], heads[:, :, 1], ALU.add))
                ve.tensor_copy(k_ext[:, :, :, HD:EXT], k_ext[:, :, :, 0:EXT - HD]).then_inc(A["k_ext"], 1)

        def act_a_values(act, t):
            act.wait_ge(A["kvp"], t.n + 1)
            act.wait_ge(A["k_read"], t.n + 1)
            wait(act, A["state"], t.n - 1)
            nc.scalar.activation(va[t.u][:, :, 0:D], KV[:, :, 2 * D:3 * D], ACT.Copy).then_inc(A["v"], 1)

        def act_a_q_high(act, t):
            act.wait_ge(A["qrot"], t.n + 1)
            wait(act, A["shift_b"], t.n - 1)
            nc.scalar.activation(q_hi[:, t.u], qr[:, t.u], ACT.Copy).then_inc(A["q_hi"], 1)

        def pool_a_q_low(pool, t):
            pool.wait_ge(A["q_hi"], t.n + 1)
            wait(pool, A["shift_b"], t.n - 1)
            nc.gpsimd.tensor_tensor(q_lo[:, t.u], qr[:, t.u], q_hi[:, t.u].bitcast(F32), ALU.subtract)\
                .then_inc(A["q_lo"], 1)

        def pool_a_key_features(pool, t):
            pool.wait_ge(A["k_ext"], t.n + 1)
            wait(pool, A["state"], t.n - 1)
            for d in range(1, ND):
                i = nc.gpsimd.tensor_tensor(kf[:, t.u, :, d].rearrange("p s (h e) -> p s h e", e=HD),
                                            k_ext[:, :, :, 0:HD], k_ext[:, :, :, d:d + HD], ALU.mult)
            i.then_inc(A["kf"], 1)

        def dve_a_query_features(dve, t, k):
            dve.wait_ge(A["shift_a" if k == 0 else "shift_b"], t.n + 1)
            if k == 0:
                wait(dve, A["outp"], t.n - 1)
            nc.vector.tensor_tensor(qf[:, t.u, 1 + 2 * k:3 + 2 * k], QS, bc(qr[:, t.u], 1, [P, 2, T]), ALU.mult)\
                .then_inc(A["qf_a" if k == 0 else "qf_b"], 1)

        def dve_a_state(dve, t):
            ve = nc.vector
            dve.wait_ge(A["state"], t.n + 1)
            wait(dve, A["outp"], t.n - 1)
            half = lambda ap: ap.rearrange("p (b f) w -> p b f w", b=2)
            ve.tensor_tensor(half(rmat[:, t.u, 0:NF, 0:D]), ST[:, :, :, 0:D], half(mask[:, :, 0:D]), ALU.mult)
            ve.tensor_tensor(half(rmat[:, t.u, 0:NF, D:VW]), ST[:, :, :, D:D + 1].to_broadcast([P, 2, NF // 2, HEADS]),
                             half(mask[:, :, D:VW]), ALU.mult).then_inc(A["rmat"], 1)

        def act_a_sums(act, t):
            act.wait_ge(A["state"], t.n + 1)
            wait(act, A["out_read"], t.n - 1)
            nc.scalar.activation(sums[:, t.u], SUMS, ACT.Copy).then_inc(A["sums"], 1)

        def dve_a_normalise(dve, t, own):
            ve = nc.vector
            dve.wait_ge(A["outp"], t.n + 1)
            dve.wait_ge(A["sums"], t.n + 1)
            ve.tensor_tensor(total[:], OUT, bc(sums[:, t.u], 1, [P, BS, VW]), ALU.add).then_inc(A["out_read"], 1)
            dve.wait_ge(A["out_read"], t.n + 1)
            own.done(ve.reciprocal(rz[:], total[:, :, D:VW]))
            wait(dve, A["atTp"], t.n - 1)
            heads = lambda ap: ap.rearrange("p s (h e) -> p s h e", e=HD)
            ve.tensor_tensor(heads(at[:, t.u]), heads(total[:, :, 0:D]), bc(rz[:], 3, [P, BS, HEADS, HD]), ALU.mult)\
                .then_inc(A["at"], 1)

        def dve_a_residual(dve, t):
            dve.wait_ge(A["yp"], t.n + 1)
            dve.wait_ge(A[f"xr_in{t.u}"], 16 * (t.h + 1))
            dve.wait_ge(A[f"stored{t.u}"], 16 * (t.h + 1))
            nc.vector.tensor_tensor(xs[:, t.u], Y, xr[:, t.u], ALU.add).then_inc(A["xo"], 1)

        def act_a_linear_q(act, t):
            act.wait_ge(A["qrot"], t.n + 1)
            wait(act, A["outp"], t.n - 1)
            nc.scalar.activation(qf[:, t.u, 0], qr[:, t.u], ACT.Square)
            nc.scalar.activation(qf[:, t.u, ND], qr[:, t.u], ACT.Copy).then_inc(A["sq"], 1)

        def act_a_keys(act, t):
            act.wait_ge(A["k_ext"], t.n + 1)
            wait(act, A["state"], t.n - 1)
            keys = k_ext[:, :, :, 0:HD]
            for f, func in ((0, ACT.Square), (ND, ACT.Copy)):
                i = nc.scalar.activation(kf[:, t.u, :, f].rearrange("p s (h e) -> p s h e", e=HD), keys, func)
            i.then_inc(A["k_lin"], 1)

        def act_a_hT(act, t):
            act.wait_ge(A["hTp"], t.n + 1)
            wait(act, A["kvp"], t.n - 1)
            nc.scalar.activation(hT[:, t.u], T0, ACT.Identity, bias=lnb[:], scale=lnw[:]).then_inc(A["hT"], 1)

        def act_a_atT(act, t):
            act.wait_ge(A["atTp"], t.n + 1)
            wait(act, A["yp"], t.n - 1)
            nc.scalar.activation(atT[:, t.u], AT, ACT.Copy).then_inc(A["atT"], 1)

        def pe_a_hT(pe, t):
            pe.wait_ge(A["hn"], t.n + 1)
            wait(pe, A["q_read"], t.n)
            for s in range(BS):
                i = nc.tensor.transpose(T0[:, s * P:(s + 1) * P], hn[:, t.u, s], ident[:])
            i.then_inc(A["hTp"], 1)

        def pe_a_qkv(pe, t):
            pe.wait_ge(A["hT"], t.n + 1)
            for w in range(2):
                i = nc.tensor.matmul(Q[:, w], wq[:, w], hT[:, t.u], start=True, stop=True)
            i.then_inc(A["qp"], 1)
            wait(pe, A["v"], t.n)
            for s in range(BS):
                i = nc.tensor.matmul(KV[:, s, 0:3 * D], hT[:, t.u, s * P:(s + 1) * P],
                                     wkv[:].rearrange("p w d -> p (w d)"), start=True, stop=True)
            i.then_inc(A["kvp"], 1)

        def pe_a_shift(pe, t, k):
            if k == 0:
                pe.wait_ge(A["q_lo"], t.n + 1)
                wait(pe, A["qf_b"], t.n)
            else:
                pe.wait_ge(A["qf_a"], t.n + 1)
            for w in range(2):
                nc.tensor.matmul(QS[:, w], shift[:, 2 * k + w], q_hi[:, t.u], start=True, stop=False)
                i = nc.tensor.matmul(QS[:, w], shift[:, 2 * k + w], q_lo[:, t.u], start=False, stop=True)
            i.then_inc(A["shift_a" if k == 0 else "shift_b"], 1)

        def pe_a_state(pe, t):
            pe.wait_ge(A["kf"], t.n + 1)
            pe.wait_ge(A["k_lin"], t.n + 1)
            pe.wait_ge(A["v"], t.n + 1)
            wait(pe, A["rmat"], t.n)
            wait(pe, A["out_read"], t.n - 1)
            for f in range(NF):
                for s in range(BS):
                    nc.tensor.matmul(ST[:, f // (NF // 2), f % (NF // 2)], kf[:, t.u, s, f], va[t.u][:, s, 0:D + 1],
                                     start=(s == 0), stop=(s == BS - 1))
            for s in range(BS):
                i = nc.tensor.matmul(SUMS, ones[:], va[t.u][:, s], start=(s == 0), stop=(s == BS - 1))
            i.then_inc(A["state"], 1)

        def pe_a_out(pe, t):
            pe.wait_ge(A["qf_b"], t.n + 1)
            pe.wait_ge(A["sq"], t.n + 1)
            pe.wait_ge(A["rmat"], t.n + 1)
            wait(pe, A["out_read"], t.n)
            wait(pe, A["sums"], min(BATCHES, t.n + 2) if isinstance(t.n, int) else t.n + 2)
            for s in range(BS):
                for f in range(NF):
                    i = nc.tensor.matmul(OUT[:, s], qf[:, t.u, f, s * P:(s + 1) * P], rmat[:, t.u, f],
                                     start=(f == 0), stop=(f == NF - 1))
            i.then_inc(A["outp"], 1)

        def pe_a_atT(pe, t):
            pe.wait_ge(A["at"], t.n + 1)
            wait(pe, A["atT"], t.n)
            wait(pe, A["xo"], t.n)
            for s in range(BS):
                i = nc.tensor.transpose(AT[:, s * P:(s + 1) * P], at[:, t.u, s], ident[:])
            i.then_inc(A["atTp"], 1)

        def pe_a_y(pe, t):
            pe.wait_ge(A["atT"], t.n + 1)
            for s in range(BS):
                i = nc.tensor.matmul(Y[:, s], atT[:, t.u, s * P:(s + 1) * P], wo[:], start=True, stop=True)
            i.then_inc(A["yp"], 1)

        STAGES = 5

        def stages(k, t):
            out = []
            for back in range(STAGES):
                busy = k is None or 0 <= k - back < BATCHES
                out.append(t if busy else None)
                t = t.prev()
            return out

        def sequences(eng, step):
            head = 6
            for k in range(head):
                step(stages(k, Step(k // 2, k % 2)), k)
            with eng.Fori(head // 2, BATCHES // 2) as it:
                step(stages(None, Step(it, 0)), None)
                step(stages(None, Step(it, 1)), None)
            for k in range(BATCHES, BATCHES + STAGES - 1):
                step(stages(k, Step(k // 2, k % 2)), k)

        def pe_a_step(pe, t, k):
            if t[2]:
                pe_a_shift(pe, t[2], 0)
            if t[1] and k != 1:
                pe_a_qkv(pe, t[1])
            if k == 17:
                pe_router(pe, S2, FIRST)
            if t[2]:
                pe_a_state(pe, t[2])
                pe_a_shift(pe, t[2], 1)
            if t[4]:
                pe_a_atT(pe, t[4])
            if t[3]:
                pe_a_out(pe, t[3])
            if t[0] and k != 0:
                pe_a_hT(pe, t[0])
            if k == 16:
                pe.wait_ge(A["q_read"], BATCHES)
                pe_transpose_x(pe, S2, FIRST)
            if k == 18:
                pe_transpose_c(pe, S2, FIRST)
            if t[4]:
                pe_a_y(pe, t[4])

        def dve_a_step(dve, t, k, own):
            if t[2]:
                dve_a_query_features(dve, t[2], 0)
            if t[1] and k != 1:
                for part in range(3):
                    dve_a_rotate(dve, t[1], own, part)
            if t[0] and k not in (0, 1):
                for part in range(5):
                    dve_a_norm(dve, t[0], own, part)
            if k == 16:
                dve_parts(dve_norm, range(len(NORM_AT)), dve, S2, FIRST, own)
            if k == 17:
                dve_parts(dve_split_x, range(len(SPLIT_AT)), dve, S2, FIRST, own)
                dve_parts(dve_route, range(0, 4), dve, S2, FIRST, own)
            if t[2]:
                dve_a_state(dve, t[2])
                dve_a_query_features(dve, t[2], 1)
            if k == 17:
                dve_parts(dve_route, range(4, 7), dve, S2, FIRST, own)
            if k == 18:
                dve_parts(dve_route, range(7, len(ROUTE_AT)), dve, S2, FIRST, own)
            if t[3]:
                dve_a_normalise(dve, t[3], own)
            if t[4]:
                dve_a_residual(dve, t[4])
            own.clear()

        def act_a_step(act, t, k):
            if t[2]:
                act_a_linear_q(act, t[2])
            if t[1]:
                act_a_q_high(act, t[1])
                act_a_values(act, t[1])
                act_a_keys(act, t[1])
            if k == 17:
                act_sigmoid(act, S2, FIRST)
            if t[2]:
                act_a_sums(act, t[2])
            if t[4]:
                act_a_atT(act, t[4])
            if t[0] and k != 0:
                act_a_hT(act, t[0])
            if k == 16:
                act_xTf(act, S2, FIRST)
            if k == 18:
                act_cT(act, S2, FIRST)

        def pool_a_step(pool, t, k):
            if t[1]:
                pool_a_q_low(pool, t[1])
                pool_a_key_features(pool, t[1])

        def sp_a_step(sp, t, k):
            if k == 2:
                for u in range(2):
                    sp.wait_ge(S1[f"stored{u}"], 16 * (TILES // 2 + 1))
            if t[0] and k not in (0, 1):
                sp_load_a(sp, t[0])
            if k == 16:
                for u in range(2):
                    sp.wait_ge(A[f"stored{u}"], 16 * 2)
                load_x(sp, S2, x2, FIRST)
            if t[3]:
                sp_load_r(sp, t[3])
            if t[4]:
                sp_store(sp, t[4])

        def dve_trig_part(dve, c, own):
            ve = nc.vector
            q, rest1 = th[:, 1:2], th[:, 2:3]
            pos, base, sign, turns = (trig[:, k].rearrange("p a t -> p (a t)") for k in range(4))
            if c == 0:
                dve.wait_ge(load_of["table"], 16 * 4)
                own.done(ve.tensor_scalar(q, th[:, 0:1], 1.0 / 220.0, None, ALU.mult))
                own.done(ve.tensor_copy(th_hi[:], q))
                own.done(ve.tensor_tensor(th[:, 3:4], q, th_hi[:].bitcast(F32), ALU.subtract))
                own.done(ve.scalar_tensor_tensor(out=rest1, in0=th_hi[:].bitcast(F32), scalar=-220.0,
                                                 in1=th[:, 0:1], op0=ALU.mult, op1=ALU.add))
                own.done(ve.scalar_tensor_tensor(out=rest1, in0=th[:, 3:4], scalar=-220.0, in1=rest1,
                                                 op0=ALU.mult, op1=ALU.add))
                own.done(ve.scalar_tensor_tensor(out=q, in0=rest1, scalar=1.0 / 220.0, in1=q,
                                                 op0=ALU.mult, op1=ALU.add))
            if c == 1:
                own.done(ve.tensor_scalar(base, base, q, None, ALU.mult))
                own.done(ve.tensor_tensor(pos, pos, base, ALU.mult))
            if c == 2:
                own.done(ve.tensor_scalar(turns, pos, 1.0 / TWO_PI, ROUND, ALU.mult, ALU.add))
                own.done(ve.tensor_scalar(turns, turns, ROUND, None, ALU.subtract))
            if 3 <= c <= 5:
                own.done(ve.scalar_tensor_tensor(out=pos, in0=turns, scalar=-TWO_PI_PARTS[c - 3], in1=pos,
                                                 op0=ALU.mult, op1=ALU.add))
            if c == 6:
                ve.tensor_scalar(pos, pos, PI_BELOW, -PI_BELOW, ALU.min, ALU.max).then_inc(trig_ready, 1)
            if c == 9:
                dve.wait_ge(sin_ready, 1)
                own.done(ve.tensor_tensor(turns, turns, turns, ALU.mult))
                half, sg, sn = trig[:, 3], trig[:, 2], trig[:, 1]
                k_view = lambda ap: ap[:, 0].rearrange("p (s d) -> p s d", s=BS)
                ve.tensor_scalar(tab_k[:, :, 0], k_view(half), -2.0, 1.0, ALU.mult, ALU.add)
                ve.tensor_scalar(tab_q[:, 0], half[:, 1], -2.0, 1.0, ALU.mult, ALU.add)
                ve.tensor_tensor(tab_k[:, :, 1], k_view(sn), k_view(sg), ALU.mult)
                own.done(ve.tensor_tensor(tab_q[:, 1], sn[:, 1], sg[:, 1], ALU.mult))

        def act_high_part(act, raw, hi, loads, ready, k):
            a, b = PIECES[k]
            act.wait_ge(load_of[f"{loads}{k}"], 16 * (2 if k == len(PIECES) - 1 else 1))
            nc.scalar.activation(hi[:, a:b], raw[:, a:b], ACT.Copy).then_inc(ready, 1)

        def pool_low(pool, raw, hi, lo, hi_ready, ready, k):
            a, b = PIECES[k]
            pool.wait_ge(hi_ready, k + 1)
            nc.gpsimd.tensor_tensor(lo[:, a:b], raw[:, a:b], hi[:, a:b].bitcast(F32), ALU.subtract).then_inc(ready, 1)

        def act_setup_part(act, c):
            if c == 12:
                act.wait_ge(load_of["attn"], 16 * 10)
                nc.scalar.activation(shift[:], shift_in_room, ACT.Copy).then_inc(shift_ready, 1)
            if c == 8:
                act.wait_ge(trig_ready, 1)
                nc.scalar.activation(trig[:, 1], trig[:, 0], ACT.Sin)
                nc.scalar.activation(trig[:, 3], trig[:, 0], ACT.Sin, scale=0.5).then_inc(sin_ready, 1)

        block = ctx.enter_context(nc.Block())

        def load_piece(eng, what, k, raw, routed, shared):
            a, b = PIECES[k]
            eng.dma_start(raw[:, a:min(b, RC)], routed[:, a:min(b, RC)]).then_inc(load_of[f"{what}{k}"], 16)
            if b == NC:
                eng.dma_start(raw[:, RC:NC], shared).then_inc(load_of[f"{what}{k}"], 16)

        @block.sync
        def _(sp):
            for S in (S1, A, S2):
                for u in range(2):
                    sp.sem_inc(S[f"stored{u}"], 16)
            load_x(sp, S1, x, FIRST)
            for k in range(len(PIECES)):
                load_piece(sp, "up", k, up_raw, up_w, s_up)
            for dst, src in [(trig[:, 0], pos_in), (trig[:, 1], base_in), (trig[:, 2], sign_in),
                             (th[:, 0:1], theta.partition_broadcast(P))]:
                sp.dma_start(dst, src).then_inc(load_of["table"], 16)
            for k in range(len(PIECES)):
                load_piece(sp, "down", k, down_raw, down_w, s_down)
            for dst, src in [(lnw[:], ln_w), (lnb[:], ln_b), (wq[:, 0], w_q), (wq[:, 1], w_qs), (wkv[:, 0], w_k),
                             (wkv[:, 1], w_ks), (wkv[:, 2], w_v), (wo[:], w_o), (shift_in_room, shift_in),
                             (mask[:], mask_in)]:
                sp.dma_start(dst, src).then_inc(load_of["attn"], 16)
            sp_ffn(sp, S1, x, x1)
            sequences(sp, lambda t, k: sp_a_step(sp, t, k))
            for u in range(2):
                sp.wait_ge(A[f"stored{u}"], 16 * (BATCHES // 2 + 1))
            sp_ffn(sp, S2, x2, out)
            for u in range(2):
                sp.wait_ge(S2[f"stored{u}"], 16 * (TILES // 2 + 1))

        @block.scalar
        def _(act):
            for dst, src in [(ident[:], ident_in), (rw[:], router_wT), (biasB[:], bias.partition_broadcast(P)),
                             (lower[:], lower_in), (ident2[:], ident2_in)]:
                act.dma_start(dst, src).then_inc(load_of["early"], 16)
            act.wait_ge(ones_ready, 1)
            nc.scalar.activation(warm[:], ones[:, 0:1], ACT.Sigmoid)
            act_xTf(act, S1, FIRST)
            act_high_part(act, up_raw, up_hi, "up", up_hi_ready, 0)
            act_sigmoid(act, S1, FIRST)
            for k in (1, 2, 3):
                act_high_part(act, up_raw, up_hi, "up", up_hi_ready, k)
            act.wait_ge(load_of["early"], 16 * 5)
            nc.scalar.activation(sel[:], bc(ident2[:], 2, [P, E, I_MOE]), ACT.Copy).then_inc(sel_ready, 1)
            for k in range(len(PIECES)):
                act_high_part(act, down_raw, down_hi, "down", down_hi_ready, k)
            act_cT(act, S1, FIRST)
            act_ffn(act, S1)
            act_acc(act, S1, LAST)
            sequences(act, lambda t, k: act_a_step(act, t, k))
            act.wait_ge(A["state"], BATCHES)
            act_ffn(act, S2)
            act_acc(act, S2, LAST)

        @block.gpsimd
        def _(pool):
            nc.gpsimd.memset(va[0][:, :, D:VW], 1.0)
            nc.gpsimd.memset(ones[:], 1.0).then_inc(ones_ready, 1)
            for k in range(len(PIECES)):
                pool_low(pool, up_raw, up_hi, up_lo, up_hi_ready, up_lo_ready, k)
            for k in (0, 1):
                pool_low(pool, down_raw, down_hi, down_lo, down_hi_ready, down_lo_ready, k)
            pool_ffn(pool, S1)
            pool.wait_ge(S1["down"], TILES * NC)
            nc.gpsimd.memset(va[1][:, :, D:VW], 1.0).then_inc(ones_ready, 1)
            sequences(pool, lambda t, k: pool_a_step(pool, t, k))
            pool_ffn(pool, S2)

        @block.vector
        def _(dve):
            own = Own(dve, dve_own)
            dve_parts(dve_norm, range(len(NORM_AT)), dve, S1, FIRST, own)
            dve_parts(dve_split_x, range(len(SPLIT_AT)), dve, S1, FIRST, own)
            dve.wait_ge(load_of["early"], 16 * 5)
            dve_parts(dve_route, range(len(ROUTE_AT)), dve, S1, FIRST, own)
            own.clear()
            dve_ffn(dve, S1, own)
            dve_residual(dve, S1, LAST)
            dve.wait_ge(load_of["attn"], 16 * 10)
            sequences(dve, lambda t, k: dve_a_step(dve, t, k, own))
            dve.wait_ge(A["state"], BATCHES)
            dve_ffn(dve, S2, own)
            dve_residual(dve, S2, LAST)

        @block.tensor
        def _(pe):
            pe.wait_ge(load_of["early"], 16 * 5)
            pe_transpose_x(pe, S1, FIRST)
            pe_router(pe, S1, FIRST)
            pe_transpose_c(pe, S1, FIRST)
            pe.wait_ge(sel_ready, 1)
            ffn_tiles(pe, lambda t, first, last: pe_ffn_tile(pe, S1, t, first, last))
            pe.wait_ge(load_of["attn"], 16 * 10)
            pe.wait_ge(A["q_read"], 1)
            pe.wait_ge(shift_ready, 1)
            pe_ffn_end(pe, S1)
            pe.wait_ge(S1["xo"], TILES)
            pe.wait_ge(ones_ready, 2)
            sequences(pe, lambda t, k: pe_a_step(pe, t, k))
            pe.wait_ge(A["xo"], BATCHES)
            ffn_tiles(pe, lambda t, first, last: pe_ffn_tile(pe, S2, t, first, last))
            pe_ffn_end(pe, S2)


def constants():
    ident = np.eye(P, dtype=np.float32)
    ident2 = np.concatenate([np.eye(E, dtype=np.float32)] * 2, axis=0)
    lower = np.broadcast_to(np.tril(np.ones((G, G), np.float32), -1), (P, G, G)).copy()
    rows = np.arange(P)
    shift = np.zeros((P, ND - 1, P), np.float32)
    for d in range(1, ND):
        shift[(rows // HD) * HD + (rows + d) % HD, d - 1, rows] = 1.0
    weight = np.array([0.5, 1.0, 1.0, 1.0, 0.5], np.float32) / HD
    weight = np.concatenate([weight, [np.float32(HD) ** np.float32(-0.5)]]).astype(np.float32)
    head_of_column = np.concatenate([np.arange(D) // HD, np.arange(HEADS)])
    mask = (rows[:, None, None] // HD == head_of_column[None, None, :]) * weight[None, :, None]
    pos = np.zeros((P, 2, T), np.float32)
    pos[:, 0] = rows[:, None] + P * (np.arange(T)[None, :] // P)
    pos[:, 1] = np.arange(T)[None, :]
    base4 = rope_base()
    base = np.zeros((P, 2, T), np.float32)
    base[:, 0] = base4[(np.arange(T) % HD) // 2][None, :]
    base[:, 1] = base4[(rows % HD) // 2][:, None]
    sign = np.zeros((P, 2, T), np.float32)
    sign[:, 0] = np.where(np.arange(T) % 2 == 0, -1.0, 1.0)[None, :]
    sign[:, 1] = np.where(rows % 2 == 0, -1.0, 1.0)[:, None]
    return {"ident_in": ident, "ident2_in": ident2, "lower_in": lower, "shift_in": shift,
            "mask_in": mask.astype(np.float32), "pos_in": pos, "base_in": base, "sign_in": sign}


def rope_base():
    return np.array([0.0, 0.3517848551273346, 1.3223326206207275, 4.000000953674316], np.float32)


def kernel(**inputs):
    import concourse.bacc as _bacc
    from concourse.bass_utils import run_bass_kernel_spmd as _run

    given = {k.replace("L0_attn_", "").replace("L0_ffn_", ""): np.asarray(a) for k, a in inputs.items()}
    swap = np.arange(D) ^ 1
    c = np.ascontiguousarray
    arrays = {
        "x": c(given["x"].reshape(TOKENS, D)),
        "ln_w": c(given["ln_w"].reshape(P, 1)),
        "ln_b": c(given["ln_b"].reshape(P, 1)),
        "w_q": c(given["w_q"]),
        "w_qs": c(given["w_q"][:, swap]),
        "w_k": c(given["w_kv"][:, :D]),
        "w_ks": c(given["w_kv"][:, :D][:, swap]),
        "w_v": c(given["w_kv"][:, D:]),
        "w_o": c(given["w_o"]),
        "theta": c(given["theta"].reshape(1)),
        "router_wT": c(given["router_w"].T),
        "bias": c(given["correction_bias"]),
        "up_w": c(given["up_w"].transpose(1, 0, 2).reshape(D, RC, P)),
        "down_w": c(given["down_w"].reshape(RC, P, D).transpose(1, 0, 2)),
        "s_up": c(given["shared_up_w"].reshape(D, SC, P)),
        "s_down": c(given["shared_down_w"].reshape(SC, P, D).transpose(1, 0, 2)),
        **constants(),
    }
    nc = _bacc.Bacc("TRN2", target_bir_lowering=False, num_devices=1)
    args = [nc.dram_tensor(n, a.shape, mybir.dt.from_np(a.dtype), kind="ExternalInput").ap() for n, a in arrays.items()]
    args.append(nc.dram_tensor("out", (TOKENS, D), F32, kind="ExternalOutput").ap())
    build(nc, *args)
    r = _run(nc, [arrays], core_ids=[0])
    return r.results[0]["out"].reshape(given["x"].shape)
```

```python
from contextlib import ExitStack

import concourse.bass as bass
import numpy as np
from concourse import mybir

F32 = mybir.dt.float32
F32R = mybir.dt.float32r
I32 = mybir.dt.int32
ALU = mybir.AluOpType
ACT = mybir.ActivationFunctionType
AX_X = mybir.AxisListType.X

P = 128
D = 128
TOKENS = 4096
TILE = 512
SUB = TILE // P
TILES = TOKENS // TILE
E = 64
I_MOE = 64
G = 8
GE = E // G
TOPK_GROUP = 4
SCALE = 2.5
I_SHARED = 256
RC = E * I_MOE // P
ROWS = P // E
SC = I_SHARED // P
NC = RC + SC
LAG = 5
NORM_AT = tuple(range(0, 6))
TRANSPOSE_X_AT = 8
SPLIT_AT = 10
ROUTER_AT = 11
ROUTE_AT = tuple(range(13, 33))
ROOT_AT = NC - 1
OUTPUT_AT = 11
A_NORM0_AT, A_NORM1_AT, A_NORM2_AT = 13, 18, 29
A_HT_AT = 22
A_QKV_AT = 25
A_ROTATE_AT = 26
PIECES = [(0, 8), (8, 16), (16, 24), (24, NC)]
EPS = 1e-5

T = 256
BATCHES = TOKENS // T
BS = T // P
HEADS = 16
HD = 8
ND = 5
NF = ND + 1
VW = D + HEADS
EXT = 12
NEG = -3.0e38

TWO_PI = 6.283185307179586
TWO_PI_PARTS = (6.28125, 0.0019350051879882812, 3.0199159819567e-07)
ROUND = 12582912.0
PI_BELOW = 3.1415925


def bc(ap, axis, shape):
    return ap.unsqueeze(axis).to_broadcast(shape)


class Own:

    def __init__(self, eng, sem):
        self.eng, self.sem, self.n = eng, sem, 0

    def done(self, instruction):
        self.n += 1
        instruction.then_inc(self.sem, 1)
        self.eng.wait_ge(self.sem, self.n)

    def last(self, instruction):
        self.n += 1
        instruction.then_inc(self.sem, 1)

    def ready(self):
        if self.n:
            self.eng.wait_ge(self.sem, self.n)

    def clear(self):
        if self.n:
            self.ready()
            self.eng.sem_clear(self.sem)
            self.n = 0


class Step:

    def __init__(self, h, u):
        self.h, self.u, self.n = h, u, 2 * h + u

    def next(self):
        return Step(self.h, 1) if self.u == 0 else Step(self.h + 1, 0)

    def prev(self):
        return Step(self.h, 0) if self.u == 1 else Step(self.h - 1, 1)


def wait(eng, sem, value):
    if not isinstance(value, int) or value > 0:
        eng.wait_ge(sem, value)


def rsqrt_estimate(v, y, a):
    return v.tensor_scalar(y.bitcast(I32), a.bitcast(I32), -0.5, float(0x5F3759DF), ALU.mult, ALU.add)


def rsqrt_newton(v, own, y, tmp, a):
    own.done(v.tensor_tensor(tmp, y, y, ALU.mult))
    own.done(v.scalar_tensor_tensor(out=tmp, in0=tmp, scalar=-0.5, in1=a, op0=ALU.mult, op1=ALU.mult))
    return v.scalar_tensor_tensor(out=y, in0=tmp, scalar=1.5, in1=y, op0=ALU.add, op1=ALU.mult)


def build(nc, x, ln_w, ln_b, w_q, w_qs, w_k, w_ks, w_v, w_o, theta, router_wT, bias, up_w, down_w,
          s_up, s_down, ident_in, shift_in, mask_in, pos_in, base_in, sign_in, out):
    x1 = nc.dram_tensor("x_after_ffn1", (TOKENS, D), F32).ap()
    x2 = nc.dram_tensor("x_after_attn", (TOKENS, D), F32).ap()

    with ExitStack() as ctx:
        def sb(name, shape, dt=F32):
            return ctx.enter_context(nc.sbuf_tensor(name, shape, dt))

        def sem(name):
            return ctx.enter_context(nc.semaphore(name))

        banks = ctx.enter_context(nc.psum_tensor("banks", [P, 8, 512], F32))
        bank = [banks[:, i] for i in range(8)]

        up_hi = sb("up_hi", [P, NC, P], F32R)
        up_lo = sb("up_lo", [P, NC, P], F32R)
        down_hi = sb("down_hi", [P, NC, P], F32R)
        down_lo = sb("down_lo", [P, NC, P], F32R)
        up_raw = sb("up_raw", [P, NC, P])
        down_raw = sb("down_raw", [P, NC, P])
        rw = sb("rw", [P, E])
        biasB = sb("biasB", [P, E])
        ident = sb("ident", [P, P])
        wq = sb("wq", [P, 2, D])
        wkv = sb("wkv", [P, 3, D])
        wo = sb("wo", [P, D])
        lnw = sb("lnw", [P, 1])
        lnb = sb("lnb", [P, 1])
        shift = sb("shift", [P, ND - 1, P], F32R)
        mask = sb("mask", [P, NF, VW])
        ones = sb("ones", [P, P])
        th = sb("th", [P, 8])

        xt = sb("xt", [P, 2, SUB, D])
        xo = sb("xo", [P, 2, SUB, D])
        stats = sb("stats", [P, SUB, 6])
        mv = sb("mv", [P, SUB, 2])
        small = sb("small", [P, 8, SUB])
        xn = sb("xn", [P, SUB, D])
        xTf = sb("xTf", [P, TILE])
        xT_hi = sb("xT_hi", [P, 2, TILE], F32R)
        xT_lo = sb("xT_lo", [P, 2, TILE], F32R)
        root = sb("root", [P, 2, TILE])
        scores = sb("scores", [P, SUB, E])
        sfc = sb("sfc", [P, SUB * G, GE])
        hi1 = sb("hi1", [P, SUB * G, 4])
        lo1 = sb("lo1", [P, SUB * G, 4])
        hi2 = sb("hi2", [P, SUB * G, 2])
        lo2 = sb("lo2", [P, SUB * G, 2])
        mn = sb("mn", [P, SUB * G, 2])
        gsc = sb("gsc", [P, SUB, G])
        g8 = sb("g8", [P, SUB, G])
        best4 = sb("best4", [P, SUB, G])
        grest = sb("grest", [P, SUB, G])
        gmask = sb("gmask", [P, SUB * G])
        top8 = sb("top8", [P, SUB, 8])
        rest = sb("rest", [P, SUB, E])
        comb = rest
        guess = sb("guess", [P, SUB, E])
        tmp_c = sb("tmp_c", [P, SUB, E])
        cc = sb("cc", [P, SUB, E, ROWS])
        NH, NR, NG, NP = 4, 4, 4, 6
        work = sb("work", [P, (NR + NG) * TILE])
        cuts = [work[:, k * TILE:(k + 1) * TILE] for k in range(NR + NG)]
        r, g = cuts[0:NR], cuts[NR:]
        g_hi = sb("g_hi", [P, NP, TILE], F32R)
        g_lo = sb("g_lo", [P, NP, TILE], F32R)
        acc = sb("acc", [P, TILE])
        tabs = sb("tabs", [P, 4, T])
        tab_k = tabs[:, 0:2].rearrange("p s (w d) -> p s w d", w=2)
        tab_q = tabs[:, 2:4]
        trig = sb("trig", [P, 4, 2, T])
        warm = sb("warm", [P, 1])
        th_hi = sb("th_hi", [P, 1], F32R)

        def room(raw, shapes):
            flat, at, views = raw, 0, []
            for names, dims in shapes:
                n = int(np.prod(list(dims.values())))
                views.append(flat[:, at:at + n].rearrange(f"p ({names}) -> p {names}", **dims))
                at += n
            return views

        pair = ("u s d", dict(u=2, s=BS, d=D))
        xa, xr, xs, hn, hT, q_parts, qr, k_parts = room(down_raw[:].rearrange("p c d -> p (c d)"), [
            pair, pair, pair, pair, ("u t", dict(u=2, t=T)), ("w t", dict(w=2, t=T)), ("u t", dict(u=2, t=T)),
            ("s w d", dict(s=BS, w=2, d=D))])
        qf, at, atT = room(up_raw[:].rearrange("p c d -> p (c d)"), [
            ("u f t", dict(u=2, f=NF, t=T)), pair, ("u t", dict(u=2, t=T))])
        a_stats = sb("a_stats", [P, BS, 6])
        a_mv = sb("a_mv", [P, BS, 2])
        a_small = sb("a_small", [P, 8, BS])
        k_ext = sb("k_ext", [P, BS, HEADS, EXT])
        kf, va_odd = room(work, [("u s f d", dict(u=2, s=BS, f=NF, d=D)), ("s w", dict(s=BS, w=VW))])
        va = [sb("va_even", [P, BS, VW])[:], va_odd]
        q_hi, q_lo = g_hi[:, 0:2, 0:T], g_hi[:, 2:4, 0:T]
        total = sb("total", [P, BS, VW])
        rmat, sums = room(trig[:].rearrange("p k a t -> p (k a t)"), [
            ("u f w", dict(u=2, f=NF, w=VW)), ("u w", dict(u=2, w=VW))])
        shift_raw = sb("shift_raw", [P, ND - 1, P])
        rz = sb("rz", [P, BS, HEADS])

        load_of = {n: sem(f"load_{n}") for n in
                   ["early", "table", "attn"] + [f"up{k}" for k in range(len(PIECES))] +
                   [f"down{k}" for k in range(len(PIECES))]}
        halved = sem("halved")
        up_hi_ready = sem("up_hi_ready")
        up_lo_ready = sem("up_lo_ready")
        up_lo_by_vector = sem("up_lo_by_vector")
        down_hi_ready = sem("down_hi_ready")
        down_lo_ready = sem("down_lo_ready")
        ones_ready = sem("ones_ready")
        dve_own = sem("dve_own")

        def ffn_sems(tag):
            names = ["x_in0", "x_in1", "xn", "xTp", "xTf", "xT_hi", "xsplit", "logits", "sig", "comb", "ccT", "root",
                     "up", "relu", "g", "g_hi", "g_lo", "down", "acc", "outT", "res_in0", "res_in1", "xo",
                     "stored0", "stored1"]
            return {n: sem(f"{tag}_{n}") for n in names}

        S1 = ffn_sems("f1")
        S2 = ffn_sems("f2")
        A = {n: sem(f"at_{n}") for n in
             ["x_in0", "x_in1", "xr_in0", "xr_in1", "hn", "hTp", "hT", "qp", "kvp", "v", "q_read", "k_read",
              "qrot", "k_ext", "k_lin", "sq", "kf", "shift_a", "shift_b", "qf_a", "qf_b", "state", "sums",
              "rmat", "out_read", "q_hi", "q_lo",
              "outp", "at", "atTp", "atT", "yp", "xo", "stored0", "stored1"]}
        trig_ready = sem("trig_ready")
        sin_ready = sem("sin_ready")
        shift_ready = sem("shift_ready")

        ACC = [bank[1], bank[7]]
        XT = bank[0]
        LG = bank[2]
        CT = bank[2]
        H = [bank[4], bank[5], bank[6], bank[3]]

        FIRST, LAST = Step(0, 0), Step(TILES // 2 - 1, 1)

        def load_x(sp, S, src, t):
            wait(sp, S["xn"], t.n - 1)
            sp.dma_start(xt[:, t.u], src_tile(src, t)).then_inc(S[f"x_in{t.u}"], 16)

        def load_residual(sp, S, src, t):
            sp.wait_ge(S[f"stored{t.u}"], 16 * (t.h + 1))
            sp.dma_start(xo[:, t.u], src_tile(src, t)).then_inc(S[f"res_in{t.u}"], 16)

        def src_tile(ap, t):
            return ap.rearrange("(n p) d -> p n d", p=P)[:, bass.ds(t.n * SUB, SUB), :]

        def store_x(sp, S, dst, t):
            sp.wait_ge(S["xo"], t.n + 1)
            sp.dma_start(src_tile(dst, t), xo[:, t.u]).then_inc(S[f"stored{t.u}"], 16)

        def sp_ffn_tile(sp, S, src, dst, t, first, last):
            if not last:
                load_x(sp, S, src, t.next())
            load_residual(sp, S, src, t)
            if not first:
                store_x(sp, S, dst, t.prev())
            if last and S is S1:
                sp.wait_ge(S1["stored0"], 16 * 2)
                sp_load_a(sp, Step(0, 0))
                sp_load_a(sp, Step(0, 1))
                sp.wait_ge(S1["stored1"], 16 * 2)
                sp_load_a(sp, Step(1, 0))

        def dve_norm(dve, S, t, own, part):
            ve = nc.vector
            rstd, tmp, var = small[:, 1], small[:, 2], small[:, 0]
            own.ready()
            if part == 0:
                dve.wait_ge(S[f"x_in{t.u}"], 16 * (t.h + 1))
                for s in range(SUB):
                    i = ve.bn_stats(out=stats[:, s], in_=xt[:, t.u, s])
                own.last(i)
            if part == 1:
                for s in range(SUB):
                    i = ve.bn_aggr(out=mv[:, s], in_=stats[:, s])
                own.done(i)
                own.done(ve.tensor_scalar(var, mv[:, :, 1], EPS, None, ALU.add))
                own.last(rsqrt_estimate(ve, rstd, var))
            if part in (2, 3, 4):
                own.last(rsqrt_newton(ve, own, rstd, tmp, var))
            if part == 5:
                wait(dve, S["xTp"], t.n)
                for s in range(SUB):
                    i = ve.tensor_scalar(xn[:, s], xt[:, t.u, s], mv[:, s, 0:1], small[:, 1, s:s + 1],
                                         ALU.subtract, ALU.mult)
                i.then_inc(S["xn"], 1)

        def dve_split_x(dve, S, t):
            ve = nc.vector
            dve.wait_ge(S["xT_hi"], t.n + 1)
            wait(dve, S["up"], (t.n - 1) * NC)
            ve.tensor_tensor(xT_lo[:, t.u], xTf[:], xT_hi[:, t.u].bitcast(F32), ALU.subtract).then_inc(S["xsplit"], 1)

        def dve_route(dve, S, t, own, part):
            ve = nc.vector
            m = sfc[:].rearrange("p (s g) e -> p s (g e)", s=SUB)
            own.ready()
            if part == 0:
                dve.wait_ge(S["sig"], t.n + 1)
                own.last(ve.tensor_tensor(m, scores[:], bc(biasB[:], 1, [P, SUB, E]), ALU.add))
            if part == 1:
                ve.tensor_tensor(hi1[:], sfc[:, :, 0:4], sfc[:, :, 4:8], ALU.max)
                own.last(ve.tensor_tensor(lo1[:], sfc[:, :, 0:4], sfc[:, :, 4:8], ALU.min))
            if part == 2:
                ve.tensor_tensor(hi2[:], hi1[:, :, 0:2], hi1[:, :, 2:4], ALU.max)
                ve.tensor_tensor(mn[:], hi1[:, :, 0:2], hi1[:, :, 2:4], ALU.min)
                own.done(ve.tensor_tensor(lo2[:], lo1[:, :, 0:2], lo1[:, :, 2:4], ALU.max))
                own.last(ve.tensor_tensor(lo2[:], lo2[:], mn[:], ALU.max))
            if part == 3:
                ve.tensor_tensor(hi1[:, :, 0:1], hi2[:, :, 0:1], hi2[:, :, 1:2], ALU.max)
                ve.tensor_tensor(mn[:, :, 0:1], hi2[:, :, 0:1], hi2[:, :, 1:2], ALU.min)
                own.done(ve.tensor_tensor(lo1[:, :, 0:1], lo2[:, :, 0:1], lo2[:, :, 1:2], ALU.max))
                own.done(ve.tensor_tensor(lo1[:, :, 0:1], lo1[:, :, 0:1], mn[:, :, 0:1], ALU.max))
                gs = gsc[:].rearrange("p s g -> p (s g)").unsqueeze(2)
                own.last(ve.tensor_tensor(gs, hi1[:, :, 0:1], lo1[:, :, 0:1], ALU.add))
            if part == 4:
                for s in range(SUB):
                    i = ve.max(g8[:, s], gsc[:, s])
                own.done(i)
                own.last(ve.tensor_copy(best4[:, :, 0:TOPK_GROUP], g8[:, :, 0:TOPK_GROUP]))
            if part == 5:
                for s in range(SUB):
                    i = ve.match_replace(out=grest[:, s], in_to_replace=best4[:, s], in_values=gsc[:, s],
                                         imm_value=NEG)
                own.done(i)
                own.last(ve.tensor_scalar(gmask[:], grest[:].rearrange("p s g -> p (s g)"), NEG / 2, None, ALU.is_lt))
            if part == 6:
                own.last(ve.tensor_tensor(sfc[:], sfc[:], bc(gmask[:], 2, [P, SUB * G, GE]), ALU.mult))
            if part == 7:
                for s in range(SUB):
                    i = ve.max(top8[:, s], m[:, s])
                own.last(i)
            if part == 8:
                for s in range(SUB):
                    i = ve.match_replace(out=rest[:, s], in_to_replace=top8[:, s], in_values=m[:, s], imm_value=NEG)
                own.last(i)
            if part == 9:
                own.done(ve.scalar_tensor_tensor(out=comb[:], in0=rest[:], scalar=NEG / 2, in1=scores[:],
                                                 op0=ALU.is_lt, op1=ALU.mult))
                own.last(ve.tensor_reduce(out=small[:, 3], in_=comb[:], axis=AX_X, op=ALU.add))
            if part == 10:
                own.done(ve.tensor_scalar(small[:, 3], small[:, 3], 1e-20, None, ALU.add))
                own.done(ve.reciprocal(small[:, 4], small[:, 3]))
                own.last(ve.scalar_tensor_tensor(out=comb[:], in0=comb[:], scalar=0.5 * SCALE,
                                                 in1=bc(small[:, 4], 2, [P, SUB, E]), op0=ALU.mult, op1=ALU.mult))
            y, u, w = guess[:], tmp_c[:], comb[:]
            if part == 11:
                own.last(rsqrt_estimate(ve, y, w))
            if part in (12, 15):
                own.last(ve.tensor_tensor(u, w, y, ALU.mult))
            if part == 13:
                own.last(ve.scalar_tensor_tensor(out=u, in0=u, scalar=-0.5, in1=y, op0=ALU.mult, op1=ALU.mult))
            if part == 14:
                own.last(ve.scalar_tensor_tensor(out=y, in0=u, scalar=1.5, in1=y, op0=ALU.add, op1=ALU.mult))
            if part == 16:
                own.last(ve.tensor_tensor(u, u, y, ALU.mult))
            if part == 17:
                own.last(ve.scalar_tensor_tensor(out=u, in0=u, scalar=-10.0 / 3.0, in1=u,
                                                 op0=ALU.add, op1=ALU.mult))
            if part == 18:
                own.last(ve.scalar_tensor_tensor(out=y, in0=u, scalar=5.0, in1=y, op0=ALU.add, op1=ALU.mult))
            if part == 19:
                wait(dve, S["ccT"], t.n)
                twice = lambda ap: bc(ap, 3, [P, SUB, E, ROWS])
                ve.scalar_tensor_tensor(out=cc[:], in0=twice(w), scalar=0.375, in1=twice(y),
                                        op0=ALU.mult, op1=ALU.mult).then_inc(S["comb"], 1)

        def dve_residual(dve, S, t):
            dve.wait_ge(S["outT"], t.n + 1)
            dve.wait_ge(S[f"res_in{t.u}"], 16 * (t.h + 1))
            x_out = xo[:, t.u].rearrange("p s d -> p (s d)")
            nc.vector.tensor_tensor(x_out, XT, x_out, ALU.add).then_inc(S["xo"], 1)

        def buf(t, c, count):
            return (t.u * NC + c) % count

        def parts_free(eng, S, t, c):
            t, c = (t, c - NP) if c >= NP else (t.prev(), max(k for k in range(NC) if k % NP == c % NP))
            wait(eng, S["down"], t.n * NC + c + 1)

        def dve_relu(dve, S, t, c):
            n = t.n * NC + c
            if c == 0:
                dve.wait_ge(S["root"], t.n + 1)
            dve.wait_ge(S["up"], n + 1)
            wait(dve, S["g_hi"], n + 1 - NR)
            if c < RC:
                i = nc.vector.scalar_tensor_tensor(out=r[buf(t, c, NR)], in0=H[buf(t, c, NH)], scalar=0.0,
                                                   in1=root[:, t.u], op0=ALU.max, op1=ALU.mult)
            else:
                i = nc.vector.tensor_scalar(r[buf(t, c, NR)], H[buf(t, c, NH)], 0.0, None, ALU.max)
            i.then_inc(S["relu"], 1)

        def dve_ffn_tile(dve, S, t, first, last, own):
            for c in range(NC):
                dve_relu(dve, S, t, c)
                if last and S is S1:
                    dve_trig_part(dve, c, own)
                    for start, sequence in ((A_NORM0_AT, Step(0, 0)), (A_NORM1_AT, Step(0, 1)), (A_NORM2_AT, Step(1, 0))):
                        if start <= c < start + A_NORM_PARTS:
                            dve_a_norm(dve, sequence, own, c - start)
                    if A_ROTATE_AT <= c < A_ROTATE_AT + A_ROTATE_PARTS:
                        dve_a_rotate(dve, FIRST, own, c - A_ROTATE_AT)
                if c == OUTPUT_AT and not first:
                    dve_residual(dve, S, t.prev())
                if last:
                    continue
                if c in NORM_AT:
                    dve_norm(dve, S, t.next(), own, NORM_AT.index(c))
                if c == SPLIT_AT:
                    dve_split_x(dve, S, t.next())
                if c in ROUTE_AT:
                    dve_route(dve, S, t.next(), own, ROUTE_AT.index(c))
            own.clear()

        def dve_parts(part_of, parts, dve, S, t, own):
            for part in parts:
                part_of(dve, S, t, own, part)

        def act_xTf(act, S, t):
            act.wait_ge(S["xTp"], t.n + 1)
            wait(act, S["logits"], t.n)
            wait(act, S["xsplit"], t.n)
            nc.scalar.activation(xTf[:], XT, ACT.Copy).then_inc(S["xTf"], 1)
            wait(act, S["up"], (t.n - 1) * NC)
            nc.scalar.activation(xT_hi[:, t.u], XT, ACT.Copy).then_inc(S["xT_hi"], 1)

        def act_sigmoid(act, S, t):
            act.wait_ge(S["logits"], t.n + 1)
            wait(act, S["comb"], t.n)
            nc.scalar.activation(scores[:].rearrange("p s e -> p (s e)"), LG[:, 0:SUB * E],
                                 ACT.Sigmoid).then_inc(S["sig"], 1)

        def act_root(act, S, t):
            act.wait_ge(S["ccT"], t.n + 1)
            wait(act, S["relu"], (t.n - 1) * NC)
            nc.scalar.activation(root[:, t.u], CT, ACT.Copy).then_inc(S["root"], 1)

        def act_acc(act, S, t):
            act.wait_ge(S["down"], (t.n + 1) * NC)
            nc.scalar.activation(acc[:], ACC[t.u], ACT.Copy).then_inc(S["acc"], 1)

        def act_square(act, S, t, c):
            n = t.n * NC + c
            act.wait_ge(S["relu"], n + 1)
            wait(act, S["g_lo"], n + 1 - NG)
            nc.scalar.activation(g[buf(t, c, NG)], r[buf(t, c, NR)], ACT.Square).then_inc(S["g"], 1)
            parts_free(act, S, t, c)
            nc.scalar.activation(g_hi[:, c % NP], r[buf(t, c, NR)], ACT.Square).then_inc(S["g_hi"], 1)

        def act_ffn_tile(act, S, t, first, last):
            for c in range(NC):
                act_square(act, S, t, c)
                if last and S is S1:
                    act_table_part(act, c)
                if c == LAG and not first:
                    act_acc(act, S, t.prev())
                if last:
                    if S is S1 and c == A_HT_AT:
                        act.wait_ge(load_of["attn"], 16 * 10)
                        act_a_hT(act, FIRST)
                    continue
                if c == TRANSPOSE_X_AT:
                    act_xTf(act, S, t.next())
                if c == ROUTER_AT:
                    act_sigmoid(act, S, t.next())
                if c == ROOT_AT:
                    act_root(act, S, t.next())

        def pool_ffn_tile(pool, S, t, first):
            for c in range(NC):
                n = t.n * NC + c
                pool.wait_ge(S["g_hi"], n + 1)
                parts_free(pool, S, t, c)
                b = c % NP
                nc.gpsimd.tensor_tensor(g_lo[:, b], g[buf(t, c, NG)], g_hi[:, b].bitcast(F32), ALU.subtract)\
                    .then_inc(S["g_lo"], 1)
                if first and S is S1 and c == 8:
                    pool_low(pool, down_raw, down_hi, down_lo, down_hi_ready, down_lo_ready, 3)

        def pe_transpose_x(pe, S, t):
            pe.wait_ge(S["xn"], t.n + 1)
            wait(pe, S["xo"], t.n - 2)
            for s in range(SUB):
                i = nc.tensor.transpose(XT[:, s * P:(s + 1) * P], xn[:, s], ident[:])
            i.then_inc(S["xTp"], 1)

        def pe_router(pe, S, t):
            pe.wait_ge(S["xTf"], t.n + 1)
            wait(pe, S["root"], t.n)
            for s in range(SUB):
                i = nc.tensor.matmul(LG[:, s * E:(s + 1) * E], xTf[:, s * P:(s + 1) * P], rw[:],
                                     start=True, stop=True)
            i.then_inc(S["logits"], 1)

        def pe_transpose_c(pe, S, t):
            pe.wait_ge(S["comb"], t.n + 1)
            wait(pe, S["sig"], t.n + 1)
            for s in range(SUB):
                i = nc.tensor.transpose(CT[:, s * P:(s + 1) * P],
                                        cc[:, s].rearrange("p e r -> p (e r)"), ident[:])
            i.then_inc(S["ccT"], 1)

        def pe_transpose_out(pe, S, t):
            pe.wait_ge(S["acc"], t.n + 2)
            wait(pe, S["xT_hi"], min(TILES, t.n + 3) if isinstance(t.n, int) else t.n + 3)
            for s in range(SUB):
                i = nc.tensor.transpose(XT[:, s * P:(s + 1) * P], acc[:, s * P:(s + 1) * P], ident[:])
            i.then_inc(S["outT"], 1)

        def pe_down(pe, S, t, c):
            n = t.n * NC + c
            pe.wait_ge(S["g_lo"], n + 1)
            if c == 0:
                wait(pe, S["acc"], t.n)
            if isinstance(t.n, int) and t.n == 0 and S is S1 and c in starts:
                pe.wait_ge(down_lo_ready, 1 + starts.index(c))
            b = c % NP
            nc.tensor.matmul(ACC[t.u], down_hi[:, c], g_hi[:, b], start=(c == 0), stop=False)
            nc.tensor.matmul(ACC[t.u], down_hi[:, c], g_lo[:, b], start=False, stop=False)
            nc.tensor.matmul(ACC[t.u], down_lo[:, c], g_hi[:, b], start=False, stop=(c == NC - 1))\
                .then_inc(S["down"], 1)

        starts = [a for a, _ in PIECES]

        def pe_ffn_tile(pe, S, t, first, last):
            for c in range(NC):
                n = t.n * NC + c
                if c == 0:
                    pe.wait_ge(S["xsplit"], t.n + 1)
                wait(pe, S["relu"], n + 1 - NH)
                if first and S is S2 and c == NH - 1:
                    pe.wait_ge(A["xo"], BATCHES)
                if first and S is S1 and c in starts:
                    k = starts.index(c)
                    if k < 2:
                        pe.wait_ge(up_lo_by_vector, k + 1)
                    else:
                        pe.wait_ge(up_lo_ready, k - 1)
                h = H[buf(t, c, NH)]
                nc.tensor.matmul(h, up_hi[:, c], xT_hi[:, t.u], start=True, stop=False)
                nc.tensor.matmul(h, up_hi[:, c], xT_lo[:, t.u], start=False, stop=False)
                nc.tensor.matmul(h, up_lo[:, c], xT_hi[:, t.u], start=False, stop=True).then_inc(S["up"], 1)
                if c >= LAG:
                    pe_down(pe, S, t, c - LAG)
                elif not first:
                    pe_down(pe, S, t.prev(), NC - LAG + c)
                if c == 2 and first:
                    pe_transpose_c(pe, S, t)
                if c == OUTPUT_AT and not first:
                    pe_transpose_out(pe, S, t.prev())
                if last:
                    if S is S1 and c == A_HT_AT:
                        pe.wait_ge(S1["xo"], TILES - 1)
                        pe_a_hT(pe, FIRST)
                    if S is S1 and c == A_QKV_AT:
                        pe.wait_ge(S1["acc"], TILES)
                        pe.wait_ge(S1["root"], TILES)
                        pe.wait_ge(load_of["attn"], 16 * 10)
                        pe_a_qkv(pe, FIRST)
                    continue
                if c == TRANSPOSE_X_AT:
                    pe_transpose_x(pe, S, t.next())
                if c == ROUTER_AT:
                    pe_router(pe, S, t.next())
                if c == ROOT_AT:
                    pe_transpose_c(pe, S, t.next())

        def ffn_tiles(eng, step):
            step(FIRST, True, False)
            with eng.Fori(0, (TILES - 2) // 2) as it:
                step(Step(it, 1), False, False)
                step(Step(it + 1, 0), False, False)
            step(LAST, False, True)

        def sp_ffn(sp, S, src, dst):
            ffn_tiles(sp, lambda t, first, last: sp_ffn_tile(sp, S, src, dst, t, first, last))
            store_x(sp, S, dst, LAST)

        def act_ffn(act, S):
            act.sem_inc(S["acc"], 1)
            ffn_tiles(act, lambda t, first, last: act_ffn_tile(act, S, t, first, last))

        def dve_ffn(dve, S, own):
            ffn_tiles(dve, lambda t, first, last: dve_ffn_tile(dve, S, t, first, last, own))

        def pool_ffn(pool, S):
            ffn_tiles(pool, lambda t, first, last: pool_ffn_tile(pool, S, t, first))

        def pe_ffn_end(pe, S):
            for c in range(NC - LAG, NC):
                pe_down(pe, S, LAST, c)
            pe_transpose_out(pe, S, LAST)

        AT = banks[:, 3, 0:T]
        T0 = banks[:, 0, 0:T]
        Q = banks[:, 0].rearrange("p (w t) -> p w t", w=2)
        KV = banks[:, 1:3]
        Y = AT.rearrange("p (s d) -> p s d", s=BS)
        ST = banks[:, 4:6, 0:NF // 2 * (D + 1)].rearrange("p b (f w) -> p b f w", w=D + 1)
        QS = banks[:, 6].rearrange("p (w t) -> p w t", w=2)
        OUT = banks[:, 7, 0:BS * VW].rearrange("p (s w) -> p s w", s=BS)
        SUMS = banks[:, 7, BS * VW:(BS + 1) * VW]

        def tokens_of(ap, t):
            return ap.rearrange("(n p) d -> p n d", p=P)[:, bass.ds(t.n * BS, BS), :]

        def sp_load_a(sp, t):
            wait(sp, A["hn"], t.n - 1)
            sp.dma_start(xa[:, t.u], tokens_of(x1, t)).then_inc(A[f"x_in{t.u}"], 16)

        def sp_load_r(sp, t):
            wait(sp, A["xo"], t.n - 1)
            sp.dma_start(xr[:, t.u], tokens_of(x1, t)).then_inc(A[f"xr_in{t.u}"], 16)

        def sp_store(sp, t):
            sp.wait_ge(A["xo"], t.n + 1)
            sp.dma_start(tokens_of(x2, t), xs[:, t.u]).then_inc(A[f"stored{t.u}"], 16)

        A_NORM_PARTS = 5

        def dve_a_norm(dve, t, own, part):
            ve = nc.vector
            var, both, rstd, tmp = a_mv[:, :, 1], a_small[:, 0], a_small[:, 1], a_small[:, 3]
            if part == 0:
                dve.wait_ge(A[f"x_in{t.u}"], 16 * (t.h + 1))
                for s in range(BS):
                    i = ve.bn_stats(out=a_stats[:, s], in_=xa[:, t.u, s])
                own.done(i)
                for s in range(BS):
                    i = ve.bn_aggr(out=a_mv[:, s], in_=a_stats[:, s])
                own.done(i)
            if part == 1:
                own.done(ve.tensor_scalar(tmp, var, EPS, EPS, ALU.add, ALU.mult))
                own.done(ve.tensor_tensor(both, tmp, var, ALU.add))
                own.done(rsqrt_estimate(ve, rstd, both))
            if part == 2:
                own.done(rsqrt_newton(ve, own, rstd, tmp, both))
                own.done(rsqrt_newton(ve, own, rstd, tmp, both))
            if part == 3:
                own.done(rsqrt_newton(ve, own, rstd, tmp, both))
            if part == 4:
                wait(dve, A["hTp"], t.n - 1)
                for s in range(BS):
                    i = ve.tensor_scalar(hn[:, t.u, s], xa[:, t.u, s], a_mv[:, s, 0:1], a_small[:, 1, s:s + 1],
                                         ALU.subtract, ALU.mult)
                i.then_inc(A["hn"], 1)

        A_ROTATE_PARTS = 3

        def dve_a_rotate(dve, t, own, part):
            ve = nc.vector
            if part == 0:
                dve.wait_ge(A["qp"], t.n + 1)
                ve.tensor_tensor(q_parts[:], Q, tab_q, ALU.mult).then_inc(A["q_read"], 1)
                dve.wait_ge(A["q_read"], t.n + 1)
                wait(dve, A["qf_b"], t.n - 1)
                wait(dve, A["sq"], t.n - 1)
                wait(dve, A["q_lo"], t.n - 1)
                ve.tensor_tensor(qr[:, t.u], q_parts[:, 0], q_parts[:, 1], ALU.add).then_inc(A["qrot"], 1)
            if part == 1:
                dve.wait_ge(A["kvp"], t.n + 1)
                ve.tensor_tensor(k_parts[:].rearrange("p s w d -> p s (w d)"), KV[:, :, 0:2 * D],
                                 tabs[:, 0:2], ALU.mult).then_inc(A["k_read"], 1)
            if part == 2:
                dve.wait_ge(A["k_read"], t.n + 1)
                wait(dve, A["k_lin"], t.n)
                wait(dve, A["kf"], t.n)
                heads = k_parts[:].rearrange("p s w (h e) -> p s w h e", e=HD)
                own.done(ve.tensor_tensor(k_ext[:, :, :, 0:HD], heads[:, :, 0], heads[:, :, 1], ALU.add))
                ve.tensor_copy(k_ext[:, :, :, HD:EXT], k_ext[:, :, :, 0:EXT - HD]).then_inc(A["k_ext"], 1)

        def act_a_values(act, t):
            act.wait_ge(A["kvp"], t.n + 1)
            act.wait_ge(A["k_read"], t.n + 1)
            wait(act, A["state"], t.n - 1)
            nc.scalar.activation(va[t.u][:, :, 0:D], KV[:, :, 2 * D:3 * D], ACT.Copy).then_inc(A["v"], 1)

        def act_a_q_high(act, t):
            act.wait_ge(A["qrot"], t.n + 1)
            wait(act, A["shift_b"], t.n - 1)
            nc.scalar.activation(q_hi[:, t.u], qr[:, t.u], ACT.Copy).then_inc(A["q_hi"], 1)

        def pool_a_q_low(pool, t):
            pool.wait_ge(A["q_hi"], t.n + 1)
            wait(pool, A["shift_b"], t.n - 1)
            nc.gpsimd.tensor_tensor(q_lo[:, t.u], qr[:, t.u], q_hi[:, t.u].bitcast(F32), ALU.subtract)\
                .then_inc(A["q_lo"], 1)

        def pool_a_key_features(pool, t):
            pool.wait_ge(A["k_ext"], t.n + 1)
            wait(pool, A["state"], t.n - 1)
            for d in range(1, ND):
                i = nc.gpsimd.tensor_tensor(kf[:, t.u, :, d].rearrange("p s (h e) -> p s h e", e=HD),
                                            k_ext[:, :, :, 0:HD], k_ext[:, :, :, d:d + HD], ALU.mult)
            i.then_inc(A["kf"], 1)

        def dve_a_query_features(dve, t, k):
            dve.wait_ge(A["shift_a" if k == 0 else "shift_b"], t.n + 1)
            if k == 0:
                wait(dve, A["outp"], t.n - 1)
            nc.vector.tensor_tensor(qf[:, t.u, 1 + 2 * k:3 + 2 * k], QS, bc(qr[:, t.u], 1, [P, 2, T]), ALU.mult)\
                .then_inc(A["qf_a" if k == 0 else "qf_b"], 1)

        def dve_a_state(dve, t):
            ve = nc.vector
            dve.wait_ge(A["state"], t.n + 1)
            wait(dve, A["outp"], t.n - 1)
            half = lambda ap: ap.rearrange("p (b f) w -> p b f w", b=2)
            ve.tensor_tensor(half(rmat[:, t.u, 0:NF, 0:D]), ST[:, :, :, 0:D], half(mask[:, :, 0:D]), ALU.mult)
            ve.tensor_tensor(half(rmat[:, t.u, 0:NF, D:VW]), ST[:, :, :, D:D + 1].to_broadcast([P, 2, NF // 2, HEADS]),
                             half(mask[:, :, D:VW]), ALU.mult).then_inc(A["rmat"], 1)

        def act_a_sums(act, t):
            act.wait_ge(A["state"], t.n + 1)
            wait(act, A["out_read"], t.n - 1)
            nc.scalar.activation(sums[:, t.u], SUMS, ACT.Copy).then_inc(A["sums"], 1)

        def dve_a_normalise(dve, t, own):
            ve = nc.vector
            dve.wait_ge(A["outp"], t.n + 1)
            dve.wait_ge(A["sums"], t.n + 1)
            ve.tensor_tensor(total[:], OUT, bc(sums[:, t.u], 1, [P, BS, VW]), ALU.add).then_inc(A["out_read"], 1)
            dve.wait_ge(A["out_read"], t.n + 1)
            own.done(ve.reciprocal(rz[:], total[:, :, D:VW]))
            wait(dve, A["atTp"], t.n - 1)
            heads = lambda ap: ap.rearrange("p s (h e) -> p s h e", e=HD)
            ve.tensor_tensor(heads(at[:, t.u]), heads(total[:, :, 0:D]), bc(rz[:], 3, [P, BS, HEADS, HD]), ALU.mult)\
                .then_inc(A["at"], 1)

        def dve_a_residual(dve, t):
            dve.wait_ge(A["yp"], t.n + 1)
            dve.wait_ge(A[f"xr_in{t.u}"], 16 * (t.h + 1))
            dve.wait_ge(A[f"stored{t.u}"], 16 * (t.h + 1))
            nc.vector.tensor_tensor(xs[:, t.u], Y, xr[:, t.u], ALU.add).then_inc(A["xo"], 1)

        def act_a_linear_q(act, t):
            act.wait_ge(A["qrot"], t.n + 1)
            wait(act, A["outp"], t.n - 1)
            nc.scalar.activation(qf[:, t.u, 0], qr[:, t.u], ACT.Square)
            nc.scalar.activation(qf[:, t.u, ND], qr[:, t.u], ACT.Copy).then_inc(A["sq"], 1)

        def act_a_keys(act, t):
            act.wait_ge(A["k_ext"], t.n + 1)
            wait(act, A["state"], t.n - 1)
            keys = k_ext[:, :, :, 0:HD]
            for f, func in ((0, ACT.Square), (ND, ACT.Copy)):
                i = nc.scalar.activation(kf[:, t.u, :, f].rearrange("p s (h e) -> p s h e", e=HD), keys, func)
            i.then_inc(A["k_lin"], 1)

        def act_a_hT(act, t):
            act.wait_ge(A["hTp"], t.n + 1)
            wait(act, A["kvp"], t.n - 1)
            nc.scalar.activation(hT[:, t.u], T0, ACT.Identity, bias=lnb[:], scale=lnw[:]).then_inc(A["hT"], 1)

        def act_a_atT(act, t):
            act.wait_ge(A["atTp"], t.n + 1)
            wait(act, A["yp"], t.n - 1)
            nc.scalar.activation(atT[:, t.u], AT, ACT.Copy).then_inc(A["atT"], 1)

        def pe_a_hT(pe, t):
            pe.wait_ge(A["hn"], t.n + 1)
            wait(pe, A["q_read"], t.n)
            for s in range(BS):
                i = nc.tensor.transpose(T0[:, s * P:(s + 1) * P], hn[:, t.u, s], ident[:])
            i.then_inc(A["hTp"], 1)

        def pe_a_qkv(pe, t):
            pe.wait_ge(A["hT"], t.n + 1)
            for w in range(2):
                i = nc.tensor.matmul(Q[:, w], wq[:, w], hT[:, t.u], start=True, stop=True)
            i.then_inc(A["qp"], 1)
            wait(pe, A["v"], t.n)
            for s in range(BS):
                i = nc.tensor.matmul(KV[:, s, 0:3 * D], hT[:, t.u, s * P:(s + 1) * P],
                                     wkv[:].rearrange("p w d -> p (w d)"), start=True, stop=True)
            i.then_inc(A["kvp"], 1)

        def pe_a_shift(pe, t, k):
            if k == 0:
                pe.wait_ge(A["q_lo"], t.n + 1)
                wait(pe, A["qf_b"], t.n)
            else:
                pe.wait_ge(A["qf_a"], t.n + 1)
            for w in range(2):
                nc.tensor.matmul(QS[:, w], shift[:, 2 * k + w], q_hi[:, t.u], start=True, stop=False)
                i = nc.tensor.matmul(QS[:, w], shift[:, 2 * k + w], q_lo[:, t.u], start=False, stop=True)
            i.then_inc(A["shift_a" if k == 0 else "shift_b"], 1)

        def pe_a_state(pe, t):
            pe.wait_ge(A["kf"], t.n + 1)
            pe.wait_ge(A["k_lin"], t.n + 1)
            pe.wait_ge(A["v"], t.n + 1)
            wait(pe, A["rmat"], t.n)
            wait(pe, A["out_read"], t.n - 1)
            for f in range(NF):
                for s in range(BS):
                    nc.tensor.matmul(ST[:, f // (NF // 2), f % (NF // 2)], kf[:, t.u, s, f], va[t.u][:, s, 0:D + 1],
                                     start=(s == 0), stop=(s == BS - 1))
            for s in range(BS):
                i = nc.tensor.matmul(SUMS, ones[:], va[t.u][:, s], start=(s == 0), stop=(s == BS - 1))
            i.then_inc(A["state"], 1)

        def pe_a_out(pe, t):
            pe.wait_ge(A["qf_b"], t.n + 1)
            pe.wait_ge(A["sq"], t.n + 1)
            pe.wait_ge(A["rmat"], t.n + 1)
            wait(pe, A["out_read"], t.n)
            wait(pe, A["sums"], min(BATCHES, t.n + 2) if isinstance(t.n, int) else t.n + 2)
            for s in range(BS):
                for f in range(NF):
                    i = nc.tensor.matmul(OUT[:, s], qf[:, t.u, f, s * P:(s + 1) * P], rmat[:, t.u, f],
                                     start=(f == 0), stop=(f == NF - 1))
            i.then_inc(A["outp"], 1)

        def pe_a_atT(pe, t):
            pe.wait_ge(A["at"], t.n + 1)
            wait(pe, A["atT"], t.n)
            wait(pe, A["xo"], t.n)
            for s in range(BS):
                i = nc.tensor.transpose(AT[:, s * P:(s + 1) * P], at[:, t.u, s], ident[:])
            i.then_inc(A["atTp"], 1)

        def pe_a_y(pe, t):
            pe.wait_ge(A["atT"], t.n + 1)
            for s in range(BS):
                i = nc.tensor.matmul(Y[:, s], atT[:, t.u, s * P:(s + 1) * P], wo[:], start=True, stop=True)
            i.then_inc(A["yp"], 1)

        STAGES = 5

        def stages(k, t):
            out = []
            for back in range(STAGES):
                busy = k is None or 0 <= k - back < BATCHES
                out.append(t if busy else None)
                t = t.prev()
            return out

        def sequences(eng, step):
            head = 6
            for k in range(head):
                step(stages(k, Step(k // 2, k % 2)), k)
            with eng.Fori(head // 2, BATCHES // 2) as it:
                step(stages(None, Step(it, 0)), None)
                step(stages(None, Step(it, 1)), None)
            for k in range(BATCHES, BATCHES + STAGES - 1):
                step(stages(k, Step(k // 2, k % 2)), k)

        def pe_a_step(pe, t, k):
            if t[2]:
                pe_a_shift(pe, t[2], 0)
            if t[1] and k != 1:
                pe_a_qkv(pe, t[1])
            if k == 17:
                pe_router(pe, S2, FIRST)
            if t[2]:
                pe_a_state(pe, t[2])
                pe_a_shift(pe, t[2], 1)
            if t[4]:
                pe_a_atT(pe, t[4])
            if t[3]:
                pe_a_out(pe, t[3])
            if t[0] and k != 0:
                pe_a_hT(pe, t[0])
            if k == 16:
                pe.wait_ge(A["q_read"], BATCHES)
                pe_transpose_x(pe, S2, FIRST)
            if t[4]:
                pe_a_y(pe, t[4])

        def dve_a_step(dve, t, k, own):
            if t[2]:
                dve_a_query_features(dve, t[2], 0)
            if t[1] and k != 1:
                for part in range(A_ROTATE_PARTS):
                    dve_a_rotate(dve, t[1], own, part)
            if t[0] and k not in (0, 1, 2):
                for part in range(A_NORM_PARTS):
                    dve_a_norm(dve, t[0], own, part)
            if k == 16:
                dve_parts(dve_norm, range(len(NORM_AT)), dve, S2, FIRST, own)
            if k == 17:
                dve_split_x(dve, S2, FIRST)
                dve_parts(dve_route, range(0, 4), dve, S2, FIRST, own)
            if t[2]:
                dve_a_state(dve, t[2])
                dve_a_query_features(dve, t[2], 1)
            if k == 18:
                dve_parts(dve_route, range(9, 10), dve, S2, FIRST, own)
            if t[3]:
                dve_a_normalise(dve, t[3], own)
            if t[4]:
                dve_a_residual(dve, t[4])
            if k == 17:
                dve_parts(dve_route, range(4, 9), dve, S2, FIRST, own)
            if k == 18:
                dve_parts(dve_route, range(10, 14), dve, S2, FIRST, own)
            if k == 19:
                dve_parts(dve_route, range(14, len(ROUTE_AT)), dve, S2, FIRST, own)
            own.clear()

        def act_a_step(act, t, k):
            if t[2]:
                act_a_linear_q(act, t[2])
            if t[1]:
                act_a_q_high(act, t[1])
                act_a_values(act, t[1])
                act_a_keys(act, t[1])
            if k == 17:
                act_sigmoid(act, S2, FIRST)
            if t[2]:
                act_a_sums(act, t[2])
            if t[4]:
                act_a_atT(act, t[4])
            if t[0] and k != 0:
                act_a_hT(act, t[0])
            if k == 16:
                act_xTf(act, S2, FIRST)

        def pool_a_step(pool, t, k):
            if t[1]:
                pool_a_q_low(pool, t[1])
                pool_a_key_features(pool, t[1])

        def sp_a_step(sp, t, k):
            if k == 2:
                for u in range(2):
                    sp.wait_ge(S1[f"stored{u}"], 16 * (TILES // 2 + 1))
            if t[0] and k not in (0, 1, 2):
                sp_load_a(sp, t[0])
            if k == 16:
                for u in range(2):
                    sp.wait_ge(A[f"stored{u}"], 16 * 2)
                load_x(sp, S2, x2, FIRST)
            if t[3]:
                sp_load_r(sp, t[3])
            if t[4]:
                sp_store(sp, t[4])

        def dve_trig_part(dve, c, own):
            ve = nc.vector
            q, rest1 = th[:, 1:2], th[:, 2:3]
            pos, base, sign, turns = (trig[:, k].rearrange("p a t -> p (a t)") for k in range(4))
            if c == 0:
                dve.wait_ge(load_of["table"], 16 * 4)
                own.done(ve.tensor_scalar(q, th[:, 0:1], 1.0 / 220.0, None, ALU.mult))
                own.done(ve.tensor_copy(th_hi[:], q))
                own.done(ve.tensor_tensor(th[:, 3:4], q, th_hi[:].bitcast(F32), ALU.subtract))
                own.done(ve.scalar_tensor_tensor(out=rest1, in0=th_hi[:].bitcast(F32), scalar=-220.0,
                                                 in1=th[:, 0:1], op0=ALU.mult, op1=ALU.add))
                own.done(ve.scalar_tensor_tensor(out=rest1, in0=th[:, 3:4], scalar=-220.0, in1=rest1,
                                                 op0=ALU.mult, op1=ALU.add))
                own.done(ve.scalar_tensor_tensor(out=q, in0=rest1, scalar=1.0 / 220.0, in1=q,
                                                 op0=ALU.mult, op1=ALU.add))
            if c == 1:
                own.done(ve.tensor_scalar(base, base, q, None, ALU.mult))
                own.done(ve.tensor_tensor(pos, pos, base, ALU.mult))
            if c == 2:
                own.done(ve.tensor_scalar(turns, pos, 1.0 / TWO_PI, ROUND, ALU.mult, ALU.add))
                own.done(ve.tensor_scalar(turns, turns, ROUND, None, ALU.subtract))
            if 3 <= c <= 5:
                own.done(ve.scalar_tensor_tensor(out=pos, in0=turns, scalar=-TWO_PI_PARTS[c - 3], in1=pos,
                                                 op0=ALU.mult, op1=ALU.add))
            if c == 6:
                ve.tensor_scalar(pos, pos, PI_BELOW, -PI_BELOW, ALU.min, ALU.max).then_inc(trig_ready, 1)
            if c == 9:
                dve.wait_ge(sin_ready, 1)
                own.done(ve.tensor_tensor(turns, turns, turns, ALU.mult))
                half, sg, sn = trig[:, 3], trig[:, 2], trig[:, 1]
                k_view = lambda ap: ap[:, 0].rearrange("p (s d) -> p s d", s=BS)
                ve.tensor_scalar(tab_k[:, :, 0], k_view(half), -2.0, 1.0, ALU.mult, ALU.add)
                ve.tensor_scalar(tab_q[:, 0], half[:, 1], -2.0, 1.0, ALU.mult, ALU.add)
                ve.tensor_tensor(tab_k[:, :, 1], k_view(sn), k_view(sg), ALU.mult)
                own.done(ve.tensor_tensor(tab_q[:, 1], sn[:, 1], sg[:, 1], ALU.mult))

        def act_high_part(act, raw, hi, loads, ready, k):
            a, b = PIECES[k]
            act.wait_ge(load_of[f"{loads}{k}"], 16 * (2 if k == len(PIECES) - 1 else 1))
            nc.scalar.activation(hi[:, a:b], raw[:, a:b], ACT.Copy).then_inc(ready, 1)

        def dve_up_low(dve, k):
            a, b = PIECES[k]
            dve.wait_ge(up_hi_ready, k + 1)
            nc.vector.tensor_tensor(up_lo[:, a:b], up_raw[:, a:b], up_hi[:, a:b].bitcast(F32), ALU.subtract)\
                .then_inc(up_lo_by_vector, 1)

        def pool_low(pool, raw, hi, lo, hi_ready, ready, k):
            a, b = PIECES[k]
            pool.wait_ge(hi_ready, k + 1)
            nc.gpsimd.tensor_tensor(lo[:, a:b], raw[:, a:b], hi[:, a:b].bitcast(F32), ALU.subtract).then_inc(ready, 1)

        def act_table_part(act, c):
            if c == 12:
                act.wait_ge(load_of["attn"], 16 * 10)
                nc.scalar.activation(shift[:], shift_raw[:], ACT.Copy).then_inc(shift_ready, 1)
            if c == 8:
                act.wait_ge(trig_ready, 1)
                nc.scalar.activation(trig[:, 1], trig[:, 0], ACT.Sin)
                nc.scalar.activation(trig[:, 3], trig[:, 0], ACT.Sin, scale=0.5).then_inc(sin_ready, 1)

        block = ctx.enter_context(nc.Block())

        def load_piece(eng, what, k, raw, routed, shared):
            a, b = PIECES[k]
            eng.dma_start(raw[:, a:min(b, RC)], routed[:, a:min(b, RC)]).then_inc(load_of[f"{what}{k}"], 16)
            if b == NC:
                eng.dma_start(raw[:, RC:NC], shared).then_inc(load_of[f"{what}{k}"], 16)

        @block.sync
        def _(sp):
            for S in (S1, A, S2):
                for u in range(2):
                    sp.sem_inc(S[f"stored{u}"], 16)
            load_x(sp, S1, x, FIRST)
            for k in range(len(PIECES)):
                load_piece(sp, "up", k, up_raw, up_w, s_up)
            for dst, src in [(trig[:, 0], pos_in), (trig[:, 1], base_in), (trig[:, 2], sign_in),
                             (th[:, 0:1], theta.partition_broadcast(P))]:
                sp.dma_start(dst, src).then_inc(load_of["table"], 16)
            for k in range(len(PIECES)):
                load_piece(sp, "down", k, down_raw, down_w, s_down)
            for dst, src in [(lnw[:], ln_w), (lnb[:], ln_b), (wq[:, 0], w_q), (wq[:, 1], w_qs), (wkv[:, 0], w_k),
                             (wkv[:, 1], w_ks), (wkv[:, 2], w_v), (wo[:], w_o), (shift_raw[:], shift_in),
                             (mask[:], mask_in)]:
                sp.dma_start(dst, src).then_inc(load_of["attn"], 16)
            sp_ffn(sp, S1, x, x1)
            sequences(sp, lambda t, k: sp_a_step(sp, t, k))
            for u in range(2):
                sp.wait_ge(A[f"stored{u}"], 16 * (BATCHES // 2 + 1))
            sp_ffn(sp, S2, x2, out)
            for u in range(2):
                sp.wait_ge(S2[f"stored{u}"], 16 * (TILES // 2 + 1))

        @block.scalar
        def _(act):
            for dst, src in [(ident[:], ident_in), (rw[:], router_wT), (biasB[:], bias.partition_broadcast(P))]:
                act.dma_start(dst, src).then_inc(load_of["early"], 16)
            act.wait_ge(ones_ready, 1)
            nc.scalar.activation(warm[:], ones[:, 0:1], ACT.Sigmoid)
            act_high_part(act, up_raw, up_hi, "up", up_hi_ready, 0)
            act_xTf(act, S1, FIRST)
            act_high_part(act, up_raw, up_hi, "up", up_hi_ready, 1)
            act_sigmoid(act, S1, FIRST)
            for k in (2, 3):
                act_high_part(act, up_raw, up_hi, "up", up_hi_ready, k)
            for k in range(len(PIECES)):
                if k == len(PIECES) - 1:
                    act.wait_ge(load_of[f"down{k}"], 16 * 2)
                    nc.scalar.activation(down_raw[:, RC:NC], down_raw[:, RC:NC], ACT.Copy, scale=0.5)\
                        .then_inc(halved, 1)
                    act.wait_ge(halved, 1)
                act_high_part(act, down_raw, down_hi, "down", down_hi_ready, k)
            act_root(act, S1, FIRST)
            act_ffn(act, S1)
            act_acc(act, S1, LAST)
            sequences(act, lambda t, k: act_a_step(act, t, k))
            act_root(act, S2, FIRST)
            act.wait_ge(A["state"], BATCHES)
            act_ffn(act, S2)
            act_acc(act, S2, LAST)

        @block.gpsimd
        def _(pool):
            nc.gpsimd.memset(va[0][:, :, D:VW], 1.0)
            nc.gpsimd.memset(best4[:], NEG)
            nc.gpsimd.memset(ones[:], 1.0).then_inc(ones_ready, 1)
            for k in (2, 3):
                pool_low(pool, up_raw, up_hi, up_lo, up_hi_ready, up_lo_ready, k)
            for k in (0, 1, 2):
                pool_low(pool, down_raw, down_hi, down_lo, down_hi_ready, down_lo_ready, k)
            pool_ffn(pool, S1)
            pool.wait_ge(S1["down"], TILES * NC)
            nc.gpsimd.memset(va[1][:, :, D:VW], 1.0).then_inc(ones_ready, 1)
            sequences(pool, lambda t, k: pool_a_step(pool, t, k))
            pool_ffn(pool, S2)

        @block.vector
        def _(dve):
            own = Own(dve, dve_own)
            dve_parts(dve_norm, range(len(NORM_AT)), dve, S1, FIRST, own)
            dve_up_low(dve, 0)
            dve_split_x(dve, S1, FIRST)
            dve_up_low(dve, 1)
            dve.wait_ge(load_of["early"], 16 * 3)
            dve_parts(dve_route, range(len(ROUTE_AT)), dve, S1, FIRST, own)
            own.clear()
            dve_ffn(dve, S1, own)
            dve_residual(dve, S1, LAST)
            dve.wait_ge(load_of["attn"], 16 * 10)
            sequences(dve, lambda t, k: dve_a_step(dve, t, k, own))
            dve.wait_ge(A["state"], BATCHES)
            dve_ffn(dve, S2, own)
            dve_residual(dve, S2, LAST)

        @block.tensor
        def _(pe):
            pe.wait_ge(load_of["early"], 16 * 3)
            pe_transpose_x(pe, S1, FIRST)
            pe_router(pe, S1, FIRST)
            ffn_tiles(pe, lambda t, first, last: pe_ffn_tile(pe, S1, t, first, last))
            pe.wait_ge(load_of["attn"], 16 * 10)
            pe.wait_ge(A["q_read"], 1)
            pe.wait_ge(shift_ready, 1)
            pe_ffn_end(pe, S1)
            pe.wait_ge(S1["xo"], TILES)
            pe.wait_ge(ones_ready, 2)
            sequences(pe, lambda t, k: pe_a_step(pe, t, k))
            pe.wait_ge(A["rmat"], BATCHES)
            pe.wait_ge(A["qf_b"], BATCHES)
            ffn_tiles(pe, lambda t, first, last: pe_ffn_tile(pe, S2, t, first, last))
            pe_ffn_end(pe, S2)


def constants():
    ident = np.eye(P, dtype=np.float32)
    rows = np.arange(P)
    shift = np.zeros((P, ND - 1, P), np.float32)
    for d in range(1, ND):
        shift[(rows // HD) * HD + (rows + d) % HD, d - 1, rows] = 1.0
    weight = np.array([0.5, 1.0, 1.0, 1.0, 0.5], np.float32) / HD
    weight = np.concatenate([weight, [np.float32(HD) ** np.float32(-0.5)]]).astype(np.float32)
    head_of_column = np.concatenate([np.arange(D) // HD, np.arange(HEADS)])
    mask = (rows[:, None, None] // HD == head_of_column[None, None, :]) * weight[None, :, None]
    pos = np.zeros((P, 2, T), np.float32)
    pos[:, 0] = rows[:, None] + P * (np.arange(T)[None, :] // P)
    pos[:, 1] = np.arange(T)[None, :]
    base4 = rope_base()
    base = np.zeros((P, 2, T), np.float32)
    base[:, 0] = base4[(np.arange(T) % HD) // 2][None, :]
    base[:, 1] = base4[(rows % HD) // 2][:, None]
    sign = np.zeros((P, 2, T), np.float32)
    sign[:, 0] = np.where(np.arange(T) % 2 == 0, -1.0, 1.0)[None, :]
    sign[:, 1] = np.where(rows % 2 == 0, -1.0, 1.0)[:, None]
    return {"ident_in": ident, "shift_in": shift,
            "mask_in": mask.astype(np.float32), "pos_in": pos, "base_in": base, "sign_in": sign}


def rope_base():
    return np.array([0.0, 0.3517848551273346, 1.3223326206207275, 4.000000953674316], np.float32)


def kernel(**inputs):
    import concourse.bacc as _bacc
    from concourse.bass_utils import run_bass_kernel_spmd as _run

    given = {k.replace("L0_attn_", "").replace("L0_ffn_", ""): np.asarray(a) for k, a in inputs.items()}
    swap = np.arange(D) ^ 1
    c = np.ascontiguousarray
    arrays = {
        "x": c(given["x"].reshape(TOKENS, D)),
        "ln_w": c(given["ln_w"].reshape(P, 1)),
        "ln_b": c(given["ln_b"].reshape(P, 1)),
        "w_q": c(given["w_q"]),
        "w_qs": c(given["w_q"][:, swap]),
        "w_k": c(given["w_kv"][:, :D]),
        "w_ks": c(given["w_kv"][:, :D][:, swap]),
        "w_v": c(given["w_kv"][:, D:]),
        "w_o": c(given["w_o"]),
        "theta": c(given["theta"].reshape(1)),
        "router_wT": c(given["router_w"].T),
        "bias": c(given["correction_bias"]),
        "up_w": c(given["up_w"].reshape(E, D, RC, ROWS).transpose(1, 2, 0, 3).reshape(D, RC, P)),
        "down_w": c(given["down_w"].reshape(E, RC, ROWS, D).transpose(0, 2, 1, 3).reshape(P, RC, D)),
        "s_up": c(given["shared_up_w"].reshape(D, SC, P)),
        "s_down": c(given["shared_down_w"].reshape(SC, P, D).transpose(1, 0, 2)),
        **constants(),
    }
    nc = _bacc.Bacc("TRN2", target_bir_lowering=False, num_devices=1)
    args = [nc.dram_tensor(n, a.shape, mybir.dt.from_np(a.dtype), kind="ExternalInput").ap() for n, a in arrays.items()]
    args.append(nc.dram_tensor("out", (TOKENS, D), F32, kind="ExternalOutput").ap())
    build(nc, *args)
    r = _run(nc, [arrays], core_ids=[0])
    return r.results[0]["out"].reshape(given["x"].shape)
```
